# Optimizing a Trainium2 kernel written in Bass

```python
import numpy as np
import jax
import jax.numpy as jnp

def _softmax(x, axis=-1):
    return jax.nn.softmax(x, axis=axis)

def _gelu(x):
    return jax.nn.gelu(x, approximate=True)

def _silu(x):
    return jax.nn.silu(x)

def _sigmoid(x):
    return jax.nn.sigmoid(x)

def _layernorm(x, axis=-1, eps=1e-05):
    m = jnp.mean(x, axis=axis, keepdims=True)
    v = jnp.var(x, axis=axis, keepdims=True)
    return (x - m) / jnp.sqrt(v + eps)

def _scatter_add(tgt, idx, src, axis=0):
    return tgt.at[idx].add(src)

def _segment_sum(src, seg, n):
    return jax.ops.segment_sum(src, seg, n)
kernel_name = 'mk_xattn_ffn_d4_seqx_r4_9437e5'

def setup_inputs(seed: int=0):
    np.random.seed(seed)
    _w = jnp.asarray

    def _rec_inputs():
        import jax
        import jax.numpy as jnp
        _rk = jax.random.key(seed)
        x = 7.22e-05 + 1 * jax.random.normal(jax.random.fold_in(_rk, 1), (16, 256, 256), jnp.float32)
        _lenS = 256 - jax.random.randint(jax.random.fold_in(_rk, 7), (16,), 0, max(1, 256 // 4) + 1, jnp.int32)
        _lenS2 = 256 - jax.random.randint(jax.random.fold_in(_rk, 8), (16,), 0, max(1, 256 // 4) + 1, jnp.int32)
        _ctx_1024P = jax.random.normal(jax.random.fold_in(_rk, 11), (16, 16, 256), jnp.float32)
        _ctx_1024c = jax.random.dirichlet(jax.random.fold_in(_rk, 511), 0.3 * jnp.ones((16,), jnp.float32), (16, 256))
        _ctx_1024t = jnp.einsum('bsk,bkd->bsd', _ctx_1024c, _ctx_1024P)
        _ctx_1024t = _ctx_1024t * jax.lax.rsqrt(jnp.mean(jnp.square(_ctx_1024t)) + 1e-12) * 0.953939
        ctx_1024 = 4.13588e-05 + 0.999923 * (_ctx_1024t + 0.3 * jax.random.normal(jax.random.fold_in(_rk, 611), (16, 256, 256), jnp.float32))
        _validS = jnp.arange(256)[None, :] < _lenS[:, None]
        _validS2 = jnp.arange(256)[None, :] < _lenS2[:, None]
        _causal = jnp.tril(jnp.ones((256, 256), dtype=bool))
        mask_BxS2_ik0 = jnp.where(jnp.broadcast_to(_validS2[:, :], (16, 256)), 0, 1).astype(jnp.int32)
        return (x, ctx_1024, mask_BxS2_ik0)
    x, ctx_1024, mask_BxS2_ik0 = _rec_inputs()

    def _L0_xattn_setup():
        import jax, jax.numpy as jnp
        import numpy as np
        BETA = 256
        NUM_HEADS = 16
        NORM = (BETA // NUM_HEADS) ** (-0.5)
        key = jax.random.key(seed)
        ks = jax.random.split(key, 6)
        B, N = (4, 512)
        D_in_q = D_in_k = D_in_v = 256
        D_out_k = D_out_v = 256
        q = jax.random.normal(ks[0], (B, N, D_in_q), dtype=jnp.float32)
        k = jax.random.normal(ks[1], (B, N, D_in_k), dtype=jnp.float32)
        v = jax.random.normal(ks[2], (B, N, D_in_v), dtype=jnp.float32)
        Wq = jax.random.normal(ks[3], (D_out_k, D_in_q), dtype=jnp.float32) * D_in_q ** (-0.5)
        Wk = jax.random.normal(ks[4], (D_out_k, D_in_k), dtype=jnp.float32) * D_in_k ** (-0.5)
        Wv = jax.random.normal(ks[5], (D_out_v, D_in_v), dtype=jnp.float32) * D_in_v ** (-0.5)
        return {'q': q, 'k': k, 'v': v, 'Wq': Wq, 'Wk': Wk, 'Wv': Wv}
    _L0_xattn_all = _L0_xattn_setup()
    _L0_xattn_in = {k: v for k, v in _L0_xattn_all.items() if k in ('Wq', 'Wk', 'Wv')}
    del _L0_xattn_all

    def _L0_ffn_setup():
        import jax, jax.numpy as jnp
        import numpy as np
        B, T, D, E, H = (8, 512, 256, 8, 64)
        LN_EPS = 1e-05
        key = jax.random.key(seed)
        ks = jax.random.split(key, 4)
        return {'x': jax.random.normal(ks[0], (B, T, D), dtype=jnp.float32), 'Wg': jax.random.normal(ks[1], (E, D), dtype=jnp.float32) * 0.02, 'ln_scale': jnp.ones((E, D), dtype=jnp.float32), 'ln_bias': jnp.zeros((E, D), dtype=jnp.float32), 'W1': jax.random.normal(ks[2], (E, D, H), dtype=jnp.float32) * 0.02, 'b1': jnp.zeros((E, H), dtype=jnp.float32), 'W2': jax.random.normal(ks[3], (E, H, D), dtype=jnp.float32) * 0.02, 'b2': jnp.zeros((E, D), dtype=jnp.float32)}
    _L0_ffn_all = _L0_ffn_setup()
    _L0_ffn_in = {k: v for k, v in _L0_ffn_all.items() if k in ('Wg', 'ln_scale', 'ln_bias', 'W1', 'b1', 'W2', 'b2')}
    del _L0_ffn_all

    def _L1_xattn_setup():
        import jax, jax.numpy as jnp
        import numpy as np
        DIM = 256
        HEADS = 16
        HEAD_DIM = DIM // HEADS
        SCALE = HEAD_DIM ** (-0.5)
        MASK_FILL = -1000000000.0

        def layer_norm(x, gamma, beta, eps=1e-05):
            mu = jnp.mean(x, axis=-1, keepdims=True)
            var = jnp.var(x, axis=-1, keepdims=True)
            return (x - mu) * jax.lax.rsqrt(var + eps) * gamma + beta
        key = jax.random.key(seed)
        ks = jax.random.split(key, 10)
        B, N1, N2, C = (8, 64, 1024, DIM)
        s = C ** (-0.5)
        return {'x': jax.random.normal(ks[0], (B, N1, C), jnp.float32), 'kv': jax.random.normal(ks[1], (B, N2, C), jnp.float32), 'padding_mask': jax.random.randint(ks[2], (B, N2), 0, 2, jnp.int32), 'w_q': jax.random.normal(ks[3], (C, C), jnp.float32) * s, 'w_kv': jax.random.normal(ks[4], (C, 2 * C), jnp.float32) * s, 'w_proj': jax.random.normal(ks[5], (C, C), jnp.float32) * s, 'b_proj': jnp.zeros((C,), jnp.float32), 'g_x': jnp.ones((C,), jnp.float32), 'b_x': jnp.zeros((C,), jnp.float32), 'g_kv': jnp.ones((C,), jnp.float32), 'b_kv': jnp.zeros((C,), jnp.float32)}
    _L1_xattn_all = _L1_xattn_setup()
    _L1_xattn_in = {k: v for k, v in _L1_xattn_all.items() if k in ('w_q', 'w_kv', 'w_proj', 'b_proj', 'g_x', 'b_x', 'g_kv', 'b_kv')}
    del _L1_xattn_all

    def _L1_ffn_setup():
        import jax, jax.numpy as jnp
        import numpy as np
        TOP_K = 4
        key = jax.random.key(seed)
        ks = jax.random.split(key, 8)
        B, S, D, F, E, R = (2, 1024, 256, 1024, 16, 16)
        s = 0.02
        return {'x': jax.random.normal(ks[0], (B, S, D), jnp.float32), 'Wg': jax.random.normal(ks[1], (D, E), jnp.float32) * s, 'W1': jax.random.normal(ks[2], (E, D, F), jnp.float32) * s, 'A1': jax.random.normal(ks[3], (E, D, R), jnp.float32) * s, 'B1': jax.random.normal(ks[4], (E, R, F), jnp.float32) * s, 'W2': jax.random.normal(ks[5], (E, F, D), jnp.float32) * s, 'A2': jax.random.normal(ks[6], (E, F, R), jnp.float32) * s, 'B2': jax.random.normal(ks[7], (E, R, D), jnp.float32) * s}
    _L1_ffn_all = _L1_ffn_setup()
    _L1_ffn_in = {k: v for k, v in _L1_ffn_all.items() if k in ('Wg', 'W1', 'A1', 'B1', 'W2', 'A2', 'B2')}
    del _L1_ffn_all

    def _L2_xattn_setup():
        import jax, jax.numpy as jnp
        import numpy as np
        H = 16

        def _split_heads(x):
            B, S, D = x.shape
            return x.reshape(B, S, H, D // H).transpose(0, 2, 1, 3)
        key = jax.random.key(seed)
        ks = jax.random.split(key, 6)
        B, Q, K, D = (2, 512, 512, 256)
        s = 0.02
        return {'query_tokens': jax.random.normal(ks[0], (B, Q, D), jnp.float32), 'key_value_tokens': jax.random.normal(ks[1], (B, K, D), jnp.float32), 'Wq': jax.random.normal(ks[2], (D, D), jnp.float32) * s, 'bq': jnp.zeros((D,), jnp.float32), 'Wk': jax.random.normal(ks[3], (D, D), jnp.float32) * s, 'bk': jnp.zeros((D,), jnp.float32), 'Wv': jax.random.normal(ks[4], (D, D), jnp.float32) * s, 'bv': jnp.zeros((D,), jnp.float32), 'Wo': jax.random.normal(ks[5], (D, D), jnp.float32) * s, 'bo': jnp.zeros((D,), jnp.float32)}
    _L2_xattn_all = _L2_xattn_setup()
    _L2_xattn_in = {k: v for k, v in _L2_xattn_all.items() if k in ('Wq', 'bq', 'Wk', 'bk', 'Wv', 'bv', 'Wo', 'bo')}
    del _L2_xattn_all

    def _L2_ffn_setup():
        import jax, jax.numpy as jnp
        import numpy as np
        B, T, C, H, E, K, F = (2, 512, 256, 16, 8, 2, 512)
        EPS = 1e-05

        def layernorm(x, w):
            m = x.mean(-1, keepdims=True)
            v = x.var(-1, keepdims=True)
            return (x - m) * jax.lax.rsqrt(v + EPS) * w

        def attention(x, c_attn_w, c_proj_w):
            b, t, c = x.shape
            hd = c // H
            q, k, v = jnp.split(x @ c_attn_w, 3, axis=-1)
            q = q.reshape(b, t, H, hd).transpose(0, 2, 1, 3)
            k = k.reshape(b, t, H, hd).transpose(0, 2, 1, 3)
            v = v.reshape(b, t, H, hd).transpose(0, 2, 1, 3)
            att = jnp.einsum('bhqd,bhkd->bhqk', q, k) / jnp.sqrt(jnp.asarray(hd, x.dtype))
            causal = jnp.tril(jnp.ones((t, t), bool))
            att = jnp.where(causal, att, jnp.asarray(-jnp.inf, att.dtype))
            att = jax.nn.softmax(att, axis=-1)
            y = jnp.einsum('bhqk,bhkd->bhqd', att, v)
            y = y.transpose(0, 2, 1, 3).reshape(b, t, c)
            return y @ c_proj_w

        def moe_mlp(x, router_w, w1, w2):
            b, t, c = x.shape
            xf = x.reshape(-1, c)
            router_logits = xf @ router_w
            probs = jax.nn.softmax(router_logits.astype(jnp.float32), axis=-1)
            rw, sel = jax.lax.top_k(probs, K)
            rw = rw / rw.sum(axis=-1, keepdims=True)
            rw = rw.astype(x.dtype)
            w1e = w1.reshape(c, E, F).transpose(1, 0, 2)
            w2e = w2.reshape(E, F, c)
            h = jax.nn.gelu(jnp.einsum('nc,ecf->enf', xf, w1e), approximate=False)
            y_all = jnp.einsum('enf,efc->nec', h, w2e)
            y_sel = jnp.take_along_axis(y_all, sel[:, :, None], axis=1)
            y = (y_sel * rw[:, :, None]).sum(axis=1)
            return y.reshape(b, t, c)
        key = jax.random.key(seed)
        ks = jax.random.split(key, 6)
        s = 0.02
        return {'x': jax.random.normal(ks[0], (B, T, C), jnp.float32), 'ln1_w': jnp.ones((C,), jnp.float32), 'c_attn_w': jax.random.normal(ks[1], (C, 3 * C), jnp.float32) * s, 'c_proj_w': jax.random.normal(ks[2], (C, C), jnp.float32) * s, 'ln2_w': jnp.ones((C,), jnp.float32), 'router_w': jax.random.normal(ks[3], (C, E), jnp.float32) * s, 'w1': jnp.clip(jax.random.normal(ks[4], (C, E * F), jnp.float32) * s, -0.06, 0.06), 'w2': jnp.clip(jax.random.normal(ks[5], (E * F, C), jnp.float32) * s, -0.06, 0.06)}
    _L2_ffn_all = _L2_ffn_setup()
    _L2_ffn_in = {k: v for k, v in _L2_ffn_all.items() if k in ('ln1_w', 'c_attn_w', 'c_proj_w', 'ln2_w', 'router_w', 'w1', 'w2')}
    del _L2_ffn_all

    def _L3_xattn_setup():
        import jax, jax.numpy as jnp
        import numpy as np
        DIM = 256
        CTX_DIM = 256
        HEADS = 8
        DIM_HEAD = 64
        INNER = HEADS * DIM_HEAD
        EPS = 1e-05

        def _layer_norm(x, gamma, beta):
            mu = jnp.mean(x, axis=-1, keepdims=True)
            var = jnp.mean(jnp.square(x - mu), axis=-1, keepdims=True)
            return (x - mu) * jax.lax.rsqrt(var + EPS) * gamma + beta
        key = jax.random.key(seed)
        ks = jax.random.split(key, 8)
        b, n, m = (4, 512, 512)
        x = jax.random.normal(ks[0], (b, n, DIM), dtype=jnp.float32)
        context = jax.random.normal(ks[1], (b, m, CTX_DIM), dtype=jnp.float32)
        Wq = jax.random.normal(ks[2], (DIM, INNER), dtype=jnp.float32) / np.sqrt(DIM)
        Wkv = jax.random.normal(ks[3], (CTX_DIM, 2 * INNER), dtype=jnp.float32) / np.sqrt(CTX_DIM)
        Wout = jax.random.normal(ks[4], (INNER, DIM), dtype=jnp.float32) / np.sqrt(INNER)
        bout = jnp.zeros((DIM,), dtype=jnp.float32)
        g1 = jnp.ones((DIM,), dtype=jnp.float32)
        b1 = jnp.zeros((DIM,), dtype=jnp.float32)
        g2 = jnp.ones((CTX_DIM,), dtype=jnp.float32)
        b2 = jnp.zeros((CTX_DIM,), dtype=jnp.float32)
        return {'x': x, 'context': context, 'g1': g1, 'b1': b1, 'g2': g2, 'b2': b2, 'Wq': Wq, 'Wkv': Wkv, 'Wout': Wout, 'bout': bout}
    _L3_xattn_all = _L3_xattn_setup()
    _L3_xattn_in = {k: v for k, v in _L3_xattn_all.items() if k in ('g1', 'b1', 'g2', 'b2', 'Wq', 'Wkv', 'Wout', 'bout')}
    del _L3_xattn_all

    def _L3_ffn_setup():
        import jax, jax.numpy as jnp
        import numpy as np
        FP8_MAX = 448.0

        def quant_fp8(x):
            amax = jnp.max(jnp.abs(x)).astype(jnp.float32)
            scale = jnp.minimum(FP8_MAX / jnp.maximum(amax, 1e-12), FP8_MAX)
            x_fp8 = jnp.clip(x * scale, -FP8_MAX, FP8_MAX).astype(jnp.float8_e4m3fn)
            return (x_fp8, 1.0 / scale)
        key = jax.random.key(seed)
        k1, k2, k3 = jax.random.split(key, 3)
        B, S, IN, OUT = (4, 2048, 256, 256)
        input = jax.random.normal(k1, (B, S, IN), dtype=jnp.float32)
        bound = 1.0 / np.sqrt(IN)
        weight = jax.random.uniform(k2, (OUT, IN), dtype=jnp.float32, minval=-bound, maxval=bound)
        bias = jax.random.uniform(k3, (OUT,), dtype=jnp.float32, minval=-bound, maxval=bound)
        return {'input': input, 'weight': weight, 'bias': bias}
    _L3_ffn_all = _L3_ffn_setup()
    _L3_ffn_in = {k: v for k, v in _L3_ffn_all.items() if k in ('weight', 'bias')}
    del _L3_ffn_all
    return {'x': x, 'ctx_1024': ctx_1024, 'mask_BxS2_ik0': mask_BxS2_ik0, 'L0_xattn_Wq': _L0_xattn_in['Wq'], 'L0_xattn_Wk': _L0_xattn_in['Wk'], 'L0_xattn_Wv': _L0_xattn_in['Wv'], 'L0_ffn_Wg': _L0_ffn_in['Wg'], 'L0_ffn_ln_scale': _L0_ffn_in['ln_scale'], 'L0_ffn_ln_bias': _L0_ffn_in['ln_bias'], 'L0_ffn_W1': _L0_ffn_in['W1'], 'L0_ffn_b1': _L0_ffn_in['b1'], 'L0_ffn_W2': _L0_ffn_in['W2'], 'L0_ffn_b2': _L0_ffn_in['b2'], 'L1_xattn_w_q': _L1_xattn_in['w_q'], 'L1_xattn_w_kv': _L1_xattn_in['w_kv'], 'L1_xattn_w_proj': _L1_xattn_in['w_proj'], 'L1_xattn_b_proj': _L1_xattn_in['b_proj'], 'L1_xattn_g_x': _L1_xattn_in['g_x'], 'L1_xattn_b_x': _L1_xattn_in['b_x'], 'L1_xattn_g_kv': _L1_xattn_in['g_kv'], 'L1_xattn_b_kv': _L1_xattn_in['b_kv'], 'L1_ffn_Wg': _L1_ffn_in['Wg'], 'L1_ffn_W1': _L1_ffn_in['W1'], 'L1_ffn_A1': _L1_ffn_in['A1'], 'L1_ffn_B1': _L1_ffn_in['B1'], 'L1_ffn_W2': _L1_ffn_in['W2'], 'L1_ffn_A2': _L1_ffn_in['A2'], 'L1_ffn_B2': _L1_ffn_in['B2'], 'L2_xattn_Wq': _L2_xattn_in['Wq'], 'L2_xattn_bq': _L2_xattn_in['bq'], 'L2_xattn_Wk': _L2_xattn_in['Wk'], 'L2_xattn_bk': _L2_xattn_in['bk'], 'L2_xattn_Wv': _L2_xattn_in['Wv'], 'L2_xattn_bv': _L2_xattn_in['bv'], 'L2_xattn_Wo': _L2_xattn_in['Wo'], 'L2_xattn_bo': _L2_xattn_in['bo'], 'L2_ffn_ln1_w': _L2_ffn_in['ln1_w'], 'L2_ffn_c_attn_w': _L2_ffn_in['c_attn_w'], 'L2_ffn_c_proj_w': _L2_ffn_in['c_proj_w'], 'L2_ffn_ln2_w': _L2_ffn_in['ln2_w'], 'L2_ffn_router_w': _L2_ffn_in['router_w'], 'L2_ffn_w1': _L2_ffn_in['w1'], 'L2_ffn_w2': _L2_ffn_in['w2'], 'L3_xattn_g1': _L3_xattn_in['g1'], 'L3_xattn_b1': _L3_xattn_in['b1'], 'L3_xattn_g2': _L3_xattn_in['g2'], 'L3_xattn_b2': _L3_xattn_in['b2'], 'L3_xattn_Wq': _L3_xattn_in['Wq'], 'L3_xattn_Wkv': _L3_xattn_in['Wkv'], 'L3_xattn_Wout': _L3_xattn_in['Wout'], 'L3_xattn_bout': _L3_xattn_in['bout'], 'L3_ffn_weight': _L3_ffn_in['weight'], 'L3_ffn_bias': _L3_ffn_in['bias']}

def reference(x, ctx_1024, mask_BxS2_ik0, L0_xattn_Wq, L0_xattn_Wk, L0_xattn_Wv, L0_ffn_Wg, L0_ffn_ln_scale, L0_ffn_ln_bias, L0_ffn_W1, L0_ffn_b1, L0_ffn_W2, L0_ffn_b2, L1_xattn_w_q, L1_xattn_w_kv, L1_xattn_w_proj, L1_xattn_b_proj, L1_xattn_g_x, L1_xattn_b_x, L1_xattn_g_kv, L1_xattn_b_kv, L1_ffn_Wg, L1_ffn_W1, L1_ffn_A1, L1_ffn_B1, L1_ffn_W2, L1_ffn_A2, L1_ffn_B2, L2_xattn_Wq, L2_xattn_bq, L2_xattn_Wk, L2_xattn_bk, L2_xattn_Wv, L2_xattn_bv, L2_xattn_Wo, L2_xattn_bo, L2_ffn_ln1_w, L2_ffn_c_attn_w, L2_ffn_c_proj_w, L2_ffn_ln2_w, L2_ffn_router_w, L2_ffn_w1, L2_ffn_w2, L3_xattn_g1, L3_xattn_b1, L3_xattn_g2, L3_xattn_b2, L3_xattn_Wq, L3_xattn_Wkv, L3_xattn_Wout, L3_xattn_bout, L3_ffn_weight, L3_ffn_bias):
    import jax
    import jax.numpy as jnp

    def _L0_xattn_ref(q, k, v, Wq, Wk, Wv):
        import jax, jax.numpy as jnp
        import numpy as np
        BETA = 256
        NUM_HEADS = 16
        NORM = (BETA // NUM_HEADS) ** (-0.5)
        qp = jax.nn.relu(jnp.einsum('bnd,od->bno', q, Wq))
        kp = jax.nn.relu(jnp.einsum('bnd,od->bno', k, Wk))
        vp = jax.nn.relu(jnp.einsum('bnd,od->bno', v, Wv))
        B, N, D = qp.shape
        dh = D // NUM_HEADS
        qh = qp.reshape(B, N, NUM_HEADS, dh)
        kh = kp.reshape(B, N, NUM_HEADS, dh)
        vh = vp.reshape(B, N, NUM_HEADS, vp.shape[-1] // NUM_HEADS)
        E = NORM * jnp.einsum('bqhd,bkhd->bhqk', qh, kh)
        A = jax.nn.softmax(E, axis=-1)
        out = jnp.einsum('bhqk,bkhd->bqhd', A, vh)
        return out.reshape(B, N, -1)

    def _L0_ffn_ref(x, Wg, ln_scale, ln_bias, W1, b1, W2, b2):
        import jax, jax.numpy as jnp
        import numpy as np
        B, T, D, E, H = (8, 512, 256, 8, 64)
        LN_EPS = 1e-05
        Bs, Ts, Ds = x.shape
        xt = x.reshape(Bs * Ts, Ds)
        logits = xt @ Wg.T
        top1 = jnp.argmax(logits, axis=-1)
        mu = jnp.mean(xt, axis=-1, keepdims=True)
        var = jnp.mean(jnp.square(xt - mu), axis=-1, keepdims=True)
        xhat = (xt - mu) * jax.lax.rsqrt(var + LN_EPS)
        n_experts = Wg.shape[0]

        def body(y, p):
            s_e, b_e, w1, bb1, w2, bb2, eid = p
            h = jax.nn.gelu((xhat * s_e + b_e) @ w1 + bb1, approximate=False)
            out = h @ w2 + bb2
            mask = (top1 == eid)[:, None].astype(out.dtype)
            return (y + mask * out, None)
        y0 = jnp.zeros_like(xt)
        y, _ = jax.lax.scan(body, y0, (ln_scale, ln_bias, W1, b1, W2, b2, jnp.arange(n_experts)))
        return y.reshape(Bs, Ts, Ds)

    def _L1_xattn_ref(x, kv, padding_mask, w_q, w_kv, w_proj, b_proj, g_x, b_x, g_kv, b_kv):
        import jax, jax.numpy as jnp
        import numpy as np
        DIM = 256
        HEADS = 16
        HEAD_DIM = DIM // HEADS
        SCALE = HEAD_DIM ** (-0.5)
        MASK_FILL = -1000000000.0

        def layer_norm(x, gamma, beta, eps=1e-05):
            mu = jnp.mean(x, axis=-1, keepdims=True)
            var = jnp.var(x, axis=-1, keepdims=True)
            return (x - mu) * jax.lax.rsqrt(var + eps) * gamma + beta
        B, N1, C = x.shape
        N2 = kv.shape[1]
        xn = layer_norm(x, g_x, b_x)
        kvn = layer_norm(kv, g_kv, b_kv)
        q = (xn @ w_q).reshape(B, N1, HEADS, HEAD_DIM).transpose(0, 2, 1, 3)
        kv_proj = (kvn @ w_kv).reshape(B, N2, 2, HEADS, HEAD_DIM).transpose(2, 0, 3, 1, 4)
        k, v = (kv_proj[0], kv_proj[1])
        attn = jnp.einsum('bhqd,bhkd->bhqk', q, k) * SCALE
        mask = padding_mask[:, None, None, :]
        attn = jnp.where(mask == 0, MASK_FILL, attn)
        attn = jax.nn.softmax(attn, axis=-1)
        out = jnp.einsum('bhqk,bhkd->bhqd', attn, v)
        out = out.transpose(0, 2, 1, 3).reshape(B, N1, C)
        return out @ w_proj + b_proj

    def _L1_ffn_ref(x, Wg, W1, A1, B1, W2, A2, B2):
        import jax, jax.numpy as jnp
        import numpy as np
        TOP_K = 4
        Bz, S, D = x.shape
        xf = x.reshape(-1, D)
        weights = jax.nn.softmax(xf @ Wg, axis=-1)
        top_w, top_idx = jax.lax.top_k(weights, TOP_K)
        top_w = top_w / jnp.sum(top_w, axis=-1, keepdims=True)
        out = jnp.zeros_like(xf)
        for i in range(TOP_K):
            h = jax.nn.gelu(xf @ W1[i] + xf @ A1[i] @ B1[i])
            eo = h @ W2[i] + h @ A2[i] @ B2[i]
            w_i = jnp.sum(top_w * (top_idx == i), axis=-1)
            out = out + eo * w_i[:, None]
        return out.reshape(Bz, S, D)

    def _L2_xattn_ref(query_tokens, key_value_tokens, Wq, bq, Wk, bk, Wv, bv, Wo, bo):
        import jax, jax.numpy as jnp
        import numpy as np
        H = 16

        def _split_heads(x):
            B, S, D = x.shape
            return x.reshape(B, S, H, D // H).transpose(0, 2, 1, 3)
        q = _split_heads(query_tokens @ Wq + bq)
        k = _split_heads(key_value_tokens @ Wk + bk)
        v = _split_heads(key_value_tokens @ Wv + bv)
        hd = q.shape[-1]
        scores = jnp.einsum('bhqd,bhkd->bhqk', q, k) / jnp.sqrt(jnp.asarray(hd, q.dtype))
        probs = jax.nn.softmax(scores, axis=-1)
        ctx = jnp.einsum('bhqk,bhkd->bhqd', probs, v)
        B, _, Q, _ = ctx.shape
        ctx = ctx.transpose(0, 2, 1, 3).reshape(B, Q, H * hd)
        return ctx @ Wo + bo

    def _L2_ffn_ref(x, ln1_w, c_attn_w, c_proj_w, ln2_w, router_w, w1, w2):
        import jax, jax.numpy as jnp
        import numpy as np
        B, T, C, H, E, K, F = (2, 512, 256, 16, 8, 2, 512)
        EPS = 1e-05

        def layernorm(x, w):
            m = x.mean(-1, keepdims=True)
            v = x.var(-1, keepdims=True)
            return (x - m) * jax.lax.rsqrt(v + EPS) * w

        def attention(x, c_attn_w, c_proj_w):
            b, t, c = x.shape
            hd = c // H
            q, k, v = jnp.split(x @ c_attn_w, 3, axis=-1)
            q = q.reshape(b, t, H, hd).transpose(0, 2, 1, 3)
            k = k.reshape(b, t, H, hd).transpose(0, 2, 1, 3)
            v = v.reshape(b, t, H, hd).transpose(0, 2, 1, 3)
            att = jnp.einsum('bhqd,bhkd->bhqk', q, k) / jnp.sqrt(jnp.asarray(hd, x.dtype))
            causal = jnp.tril(jnp.ones((t, t), bool))
            att = jnp.where(causal, att, jnp.asarray(-jnp.inf, att.dtype))
            att = jax.nn.softmax(att, axis=-1)
            y = jnp.einsum('bhqk,bhkd->bhqd', att, v)
            y = y.transpose(0, 2, 1, 3).reshape(b, t, c)
            return y @ c_proj_w

        def moe_mlp(x, router_w, w1, w2):
            b, t, c = x.shape
            xf = x.reshape(-1, c)
            router_logits = xf @ router_w
            probs = jax.nn.softmax(router_logits.astype(jnp.float32), axis=-1)
            rw, sel = jax.lax.top_k(probs, K)
            rw = rw / rw.sum(axis=-1, keepdims=True)
            rw = rw.astype(x.dtype)
            w1e = w1.reshape(c, E, F).transpose(1, 0, 2)
            w2e = w2.reshape(E, F, c)
            h = jax.nn.gelu(jnp.einsum('nc,ecf->enf', xf, w1e), approximate=False)
            y_all = jnp.einsum('enf,efc->nec', h, w2e)
            y_sel = jnp.take_along_axis(y_all, sel[:, :, None], axis=1)
            y = (y_sel * rw[:, :, None]).sum(axis=1)
            return y.reshape(b, t, c)
        x = x + attention(layernorm(x, ln1_w), c_attn_w, c_proj_w)
        x = x + moe_mlp(layernorm(x, ln2_w), router_w, w1, w2)
        return x

    def _L3_xattn_ref(x, context, g1, b1, g2, b2, Wq, Wkv, Wout, bout):
        import jax, jax.numpy as jnp
        import numpy as np
        DIM = 256
        CTX_DIM = 256
        HEADS = 8
        DIM_HEAD = 64
        INNER = HEADS * DIM_HEAD
        EPS = 1e-05

        def _layer_norm(x, gamma, beta):
            mu = jnp.mean(x, axis=-1, keepdims=True)
            var = jnp.mean(jnp.square(x - mu), axis=-1, keepdims=True)
            return (x - mu) * jax.lax.rsqrt(var + EPS) * gamma + beta
        b, n, _ = x.shape
        m = context.shape[1]
        scale = DIM_HEAD ** (-0.5)
        xn = _layer_norm(x, g1, b1)
        cn = _layer_norm(context, g2, b2)
        q = xn @ Wq
        kv = cn @ Wkv
        k, v = jnp.split(kv, 2, axis=-1)
        q = q.reshape(b, n, HEADS, DIM_HEAD).transpose(0, 2, 1, 3)
        k = k.reshape(b, m, HEADS, DIM_HEAD).transpose(0, 2, 1, 3)
        v = v.reshape(b, m, HEADS, DIM_HEAD).transpose(0, 2, 1, 3)
        sim = jnp.einsum('bhid,bhjd->bhij', q, k) * scale
        attn = jax.nn.softmax(sim, axis=-1)
        out = jnp.einsum('bhij,bhjd->bhid', attn, v)
        out = out.transpose(0, 2, 1, 3).reshape(b, n, INNER)
        return out @ Wout + bout

    def _L3_ffn_ref(input, weight, bias):
        import jax, jax.numpy as jnp
        import numpy as np
        FP8_MAX = 448.0

        def quant_fp8(x):
            amax = jnp.max(jnp.abs(x)).astype(jnp.float32)
            scale = jnp.minimum(FP8_MAX / jnp.maximum(amax, 1e-12), FP8_MAX)
            x_fp8 = jnp.clip(x * scale, -FP8_MAX, FP8_MAX).astype(jnp.float8_e4m3fn)
            return (x_fp8, 1.0 / scale)
        prev_shape = input.shape
        x2d = input.reshape(-1, weight.shape[1])
        w_fp8, w_scale = quant_fp8(weight)
        x_fp8, x_scale = quant_fp8(x2d)
        acc = jnp.matmul(x_fp8.astype(jnp.float32), w_fp8.astype(jnp.float32).T)
        out2d = (acc * (x_scale * w_scale) + bias).astype(jnp.bfloat16)
        out = out2d.reshape(*prev_shape[:-1], weight.shape[0]).astype(input.dtype)
        return out
    x = x + _L0_xattn_ref(_layernorm(x, axis=-1), ctx_1024, ctx_1024, L0_xattn_Wq, L0_xattn_Wk, L0_xattn_Wv)
    x = x + _L0_ffn_ref(_layernorm(x, axis=-1), L0_ffn_Wg, L0_ffn_ln_scale, L0_ffn_ln_bias, L0_ffn_W1, L0_ffn_b1, L0_ffn_W2, L0_ffn_b2)
    x = x + _L1_xattn_ref(_layernorm(x, axis=-1), ctx_1024, mask_BxS2_ik0, L1_xattn_w_q, L1_xattn_w_kv, L1_xattn_w_proj, L1_xattn_b_proj, L1_xattn_g_x, L1_xattn_b_x, L1_xattn_g_kv, L1_xattn_b_kv)
    x = x + _L1_ffn_ref(_layernorm(x, axis=-1), L1_ffn_Wg, L1_ffn_W1, L1_ffn_A1, L1_ffn_B1, L1_ffn_W2, L1_ffn_A2, L1_ffn_B2)
    x = x + _L2_xattn_ref(_layernorm(x, axis=-1), ctx_1024, L2_xattn_Wq, L2_xattn_bq, L2_xattn_Wk, L2_xattn_bk, L2_xattn_Wv, L2_xattn_bv, L2_xattn_Wo, L2_xattn_bo)
    x = x + _L2_ffn_ref(_layernorm(x, axis=-1), L2_ffn_ln1_w, L2_ffn_c_attn_w, L2_ffn_c_proj_w, L2_ffn_ln2_w, L2_ffn_router_w, L2_ffn_w1, L2_ffn_w2)
    x = x + _L3_xattn_ref(_layernorm(x, axis=-1), ctx_1024, L3_xattn_g1, L3_xattn_b1, L3_xattn_g2, L3_xattn_b2, L3_xattn_Wq, L3_xattn_Wkv, L3_xattn_Wout, L3_xattn_bout)
    x = x + _L3_ffn_ref(_layernorm(x, axis=-1), L3_ffn_weight, L3_ffn_bias)
    return x

_drawn_inputs = setup_inputs


def setup_inputs(seed=0):
    import zlib

    import numpy as np

    out = dict(_drawn_inputs(seed))
    spreads = {'L0_ffn_ln_scale': (1.0, 0.6),
     'L0_ffn_ln_bias': (0.0, 0.8),
     'L0_ffn_b1': (0.0, 0.8),
     'L0_ffn_b2': (0.0, 0.1),
     'L1_xattn_b_proj': (0.0, 0.1),
     'L1_xattn_g_x': (1.0, 0.2),
     'L1_xattn_b_x': (0.0, 0.401),
     'L1_xattn_g_kv': (1.0, 0.2),
     'L1_xattn_b_kv': (0.0, 0.1),
     'L2_xattn_bq': (0.0, 0.8),
     'L2_xattn_bk': (0.0, 0.8),
     'L2_xattn_bv': (0.0, 0.308),
     'L2_xattn_bo': (0.0, 0.1),
     'L2_ffn_ln1_w': (1.0, 0.6),
     'L2_ffn_ln2_w': (1.0, 0.6),
     'L3_xattn_g1': (1.0, 0.6),
     'L3_xattn_b1': (0.0, 0.8),
     'L3_xattn_g2': (1.0, 0.2),
     'L3_xattn_b2': (0.0, 0.1),
     'L3_xattn_bout': (0.0, 0.1)}
    factors = {'L1_ffn_Wg': 2.852,
     'L1_ffn_W1': 2.703,
     'L1_ffn_A1': 8.0,
     'L1_ffn_B1': 8.0,
     'L1_ffn_A2': 8.0,
     'L1_ffn_B2': 8.0,
     'L2_xattn_Wq': 8.0,
     'L2_xattn_Wk': 8.0,
     'L3_ffn_bias': 3.586}
    for name, (base, spread) in spreads.items():
        noise = np.random.default_rng([zlib.crc32(name.encode()), seed]).standard_normal(out[name].shape)
        drawn = base * np.exp(spread * noise) if base else spread * noise
        out[name] = jnp.asarray(drawn.astype(out[name].dtype))
    for name, factor in factors.items():
        out[name] = (out[name] * factor).astype(out[name].dtype)
    return out
```

```python
import concourse.bass as bass
from concourse import mybir
from contextlib import ExitStack

P = 128
D = 256
BATCH = 16
SEQ = 256
TOK = BATCH * SEQ
TILES = TOK // P
KT = D // P
EPS = 1e-5
BIG = 1e30
MASKED = 4e9
MAXROW = 96
MASKROW = 64

F32 = mybir.dt.float32
BF16 = mybir.dt.bfloat16
I32 = mybir.dt.int32
ALU = mybir.AluOpType
ACT = mybir.ActivationFunctionType
AX = mybir.AxisListType
ADD, SUB, MUL, MAX, MIN = ALU.add, ALU.subtract, ALU.mult, ALU.max, ALU.min


class Signal:

    START = 512

    def __init__(self, ctx, nc, name, step=1):
        self.sem = ctx.enter_context(nc.semaphore(name))
        self.base, self.step, self.per = self.START, step, 1

    def begin(self, per):
        self.per = per

    def end(self, units):
        self.base += units * self.per * self.step

    def at(self, u, k):
        return u * (self.per * self.step) + (self.base + k * self.step)


def signals(ctx, nc, names, dma_names):
    s = {n: Signal(ctx, nc, n) for n in names}
    s.update({n: Signal(ctx, nc, n, 16) for n in dma_names})
    return s


ATT = ["stats_step", "var_ready", "rstd_ready", "xn_ready", "xT_ps", "xT_hi", "xT_lo", "cT_ps", "cT_hi", "cT_lo",
       "q_ps", "q_hi", "q_lo", "k_ps", "k_full", "k_hi", "k_lo", "mask_row", "v_ps", "v_sb", "s_ps", "s_max",
       "mT_ps", "m_hi", "m_lo", "st_ps", "p_ready", "pv_ps", "pv_sb", "oT_ps", "recip", "o_ready",
       "o2T_ps", "o2_hi", "o2_lo", "y_ps", "x_step", "x_done"]
ATT_DMA = ["ctx_in", "q_moved", "k_moved", "m_moved"]


class Unit:

    def __init__(self, u, half):
        self.u, self.half = u, half


def pipeline(eng, units, body):
    U = Unit
    body(U(0, 0), None, None)
    body(U(1, 1), U(0, 0), None)
    with eng.Fori(0, (units - 2) // 2) as i:
        body(U(i * 2 + 2, 0), U(i * 2 + 1, 1), U(i * 2, 0))
        body(U(i * 2 + 3, 1), U(i * 2 + 2, 0), U(i * 2 + 1, 1))
    body(None, U(units - 1, 1), U(units - 2, 0))
    body(None, None, U(units - 1, 1))


def attention(nc, g, S, cfg):
    NH, DH = cfg["heads"], D // cfg["heads"] if "dh" not in cfg else cfg["dh"]
    C = NH * DH
    CK = C // P
    NB = C // D
    wide = DH > 32
    CH = 2 if wide else 1
    NP = NH // 2
    HS = NH // 4
    W = 80 if wide else 32
    VW = DH + 1 if wide else 32
    scale = float(DH) ** -0.5
    causal, self_att, mask = bool(cfg.get("causal")), cfg.get("self"), cfg.get("mask")
    lnc = cfg.get("lnc")
    raw = not lnc and not self_att
    qbias, kbias, relu, proj = cfg.get("qbias"), cfg.get("kbias"), cfg.get("relu"), cfg.get("proj")
    SR = [(0, 96)] if not wide else [(0, 128), (0, 96)]
    TR = [(0, P)] * CH
    MC = CH - 1
    X, Y, ident, identb = g["X"], g["Y"], g["ident"], g["identb"]
    NQD = 6 if wide else 3
    per = dict(stats_step=2, var_ready=1, rstd_ready=1, xn_ready=1, q_ps=NB, q_hi=NB, q_lo=NB,
               k_ps=NB, k_full=NB, k_hi=NB, k_lo=NB, v_ps=NB, v_sb=NB, s_ps=NH, s_max=NH,
               mT_ps=2, m_hi=2, m_lo=2, st_ps=NP, p_ready=NP, pv_ps=4, pv_sb=4, oT_ps=4, recip=4, o_ready=4,
               o2T_ps=NB, o2_hi=NB, o2_lo=NB, q_moved=NQD, k_moved=NQD + (1 if mask else 0), m_moved=4)
    for n, s in S.items():
        s.begin(per.get(n, 1))

    def slots():
        order = []
        for k in range(16):
            at = []
            kq = [("k", "n", i) for i in range(NB)], [("q", "n", i) for i in range(NB)]
            if k == 0:
                at += [("stats", "n", 0), ("pv", "p", 3), ("maxT", "c", 1)]
            if k == 1:
                at += [("oT", "p", 3)] + ([("cT", "n", 0)] if raw else [])
            if k == 1:
                at += [("apply", "n", 0)]
            if k == 2:
                at += (kq[0] if raw else []) + [("xT", "n", 0)] + ([("cT", "n", 0)] if lnc else [])
            if k == 4 and proj:
                at += [("o2T", "p", i) for i in range(NB)]
            if k == 5:
                at += [("pv", "c", 0)]
            if k == 4:
                at += (kq[1] if raw else kq[0])
            if k == 6:
                at += [("y", "p", 0)]
            if k == 5:
                at += ([] if raw else kq[1])
            if k == 7:
                at += [("oT", "c", 0)]
            if k == 7:
                at += [("v", "n", i) for i in range(NB)]
            if k == 9:
                at += [("pv", "c", 1)]
            if k == 11:
                at += [("oT", "c", 1)]
            if k == 13:
                at += [("pv", "c", 2)]
            if k == 15:
                at += [("oT", "c", 2)]
            if k % (16 // NH) == 0:
                at = [("st", "c", k // (16 // NH))] + at
            if k >= 9:
                lo, hi = (k - 9) * NH // 6, (k - 9 + 1) * NH // 6
                at += [("s", "n", h) for h in range(lo, min(hi, NH))]
            if k == 12:
                at += [("maxT", "n", 0)]
            order += at
        return order

    ORDER = slots()
    TURN = (7, 0, 1)
    bank_users = [s_ for s_ in ORDER if s_[0] in ("xT", "cT", "q", "k", "v", "s", "maxT", "oT", "o2T")
                  or s_[0] == "y" and proj]
    BANK = {s_: TURN[j % 3] for j, s_ in enumerate(bank_users)}

    def release(name, u, i):
        if name in ("xT", "cT", "o2T"):
            key = {"xT": "xT", "cT": "cT", "o2T": "o2"}[name]
            return [(key + "_hi", u, i + 1), (key + "_lo", u, i + 1)]
        if name in ("q", "k") and not (name == "k" and mask):
            return [(name + "_hi", u, i + 1), (name + "_lo", u, i + 1)]
        return {"k": [("k_full", u, i + 1)], "v": [("v_sb", u, i + 1)], "s": [("s_max", u, i + 1)],
                "maxT": [("m_hi", u, i + 1), ("m_lo", u, i + 1)], "oT": [("o_ready", u, i + 1)],
                "y": [("x_done", u, 1)]}[name]

    def steps(n, c, p):
        for name, who, idx in ORDER:
            unit = {"n": n, "c": c, "p": p}[who]
            if unit is not None:
                yield name, unit, idx, ps_of(BANK.get((name, who, idx)))

    def ps_of(b):
        return None if b is None else g["ps"][:, b, :]

    with ExitStack() as ctx:
        def sb(name, shape, dt):
            return ctx.enter_context(nc.sbuf_tensor(cfg["name"] + name, shape, dt))

        wq = sb("wq", [P, 2, KT, C], BF16)
        wk = sb("wk", [P, 2, KT, C], BF16)
        wv = sb("wv", [P, 2, KT, C], BF16)
        wo = sb("wo", [P, 2, CK, D], BF16) if proj else None
        bq = sb("bq", [P, CK], F32)
        bk = sb("bk", [P, CK], F32)
        brow = sb("brow", [1, 2, D], BF16)

        QS = sb("QS", [P, 2, CH, NH, SEQ], BF16)
        KS = sb("KS", [P, 2, CH, NH, SEQ], BF16)
        VA = sb("VA", [P, 2, 2, NH, VW], F32)
        NM = sb("NM", [P, 2, 2, P], F32)
        MKI = sb("MKI", [P, BATCH * SEQ], I32) if mask else None

        def load_mask(sp):
            row = g["mask"].rearrange("(one b) s -> one (b s)", one=1)
            sp.dma_start(MKI[:], row.to_broadcast([P, BATCH * SEQ])).then_inc(S["mask_in"].sem, 16)
            sp.wait_ge(S["mask_in"].sem, S["mask_in"].at(0, 1))

        def constants(pool):
            nc.gpsimd.memset(KS[:].bitcast(F32), 0.0).then_inc(S["const_ready"].sem, 1)
            nc.gpsimd.memset(QS[:].bitcast(F32), 0.0).then_inc(S["const_ready"].sem, 1)
            nc.gpsimd.memset(VA[:], 0.0).then_inc(S["const_ready"].sem, 1)
            nc.gpsimd.memset(NM[:], 0.0).then_inc(S["const_ready"].sem, 1)

        def ones(dve):
            dve.wait_ge(S["const_ready"].sem, S["const_ready"].at(0, 4))
            nc.vector.memset(KS[MAXROW:MAXROW + 2, :, MC], 1.0).then_inc(S["const_ready"].sem, 1)
            nc.vector.memset(QS[MASKROW:MASKROW + 1, :, MC], 1.0).then_inc(S["const_ready"].sem, 1)
            nc.vector.memset(VA[:, :, :, :, DH:DH + 1], 1.0).then_inc(S["const_ready"].sem, 1)
            dve.wait_ge(S["const_ready"].sem, S["const_ready"].at(0, 7))

        S["const_ready"].begin(7)
        attention_weights(nc, g, S, cfg, wq, wk, wv, wo, bq, bk, brow, C, CK, constants, ones,
                          load_mask if mask else None)
        S["const_ready"].end(1)

        CX = sb("CX", [P, 2, 2, D], F32)
        XN = sb("XN", [P, 2, D], F32)
        CN = sb("CN", [P, 2, D], F32)
        ST6 = sb("ST6", [P, 4, 6], F32)
        MV = sb("MV", [P, 2, 4, 2], F32)
        VE = sb("VE", [P, 2, 4], F32)
        RS = sb("RS", [P, 2, 4], F32)
        xT = sb("xT", [P, 2, KT, SEQ], BF16)
        cT = xT if self_att else sb("cT", [P, 2, KT, SEQ], BF16)
        QH = sb("QH", [P, 2, CK, SEQ], BF16)
        KH = sb("KH", [P, 2, CK, SEQ], BF16)
        KF = sb("KF", [P, 2, SEQ], F32)
        MH = sb("MH", [NH // 2, 2, 2, SEQ], BF16)
        PT = sb("PT", [P, 8, 2 * SEQ], F32)
        OS = sb("OS", [P, 2, 512], F32)
        RC = sb("RC", [P, 4, 8], F32)
        O = sb("O", [P, 2, C], F32)
        oT = sb("oT", [P, 2, CK, SEQ], BF16)
        MKF = sb("MKF", [P, SEQ], F32)
        MROW = sb("MROW", [NH, SEQ], BF16)
        ps = g["ps"]
        pvb = ps[:, 6, :]

        with nc.Block() as block:
            @block.sync
            def _(sp):
                def load_ctx(u, half):
                    used = S["xn_ready" if lnc else "cT_ps"]
                    sp.wait_ge(used.sem, used.at(u - 2, 1))
                    src = g["ctx_rows"][bass.ds(u * 2, 2), :, :].rearrange("t p d -> p t d")
                    sp.dma_start(CX[:, half], src).then_inc(S["ctx_in"].sem, 16)

                def body(n, c, p):
                    for name, un, i, misc in steps(n, c, p):
                        u, half = un.u, un.half
                        if name == "stats":
                            if not self_att:
                                load_ctx(u, half)
                        elif name == "q" and i == NB - 1 or name == "k" and i == NB - 1:
                            T, src, key = (QS, QH, "q") if name == "q" else (KS, KH, "k")
                            sp.wait_ge(S[key + "_hi"].sem, S[key + "_hi"].at(u, NB))
                            sp.wait_ge(S[key + "_lo"].sem, S[key + "_lo"].at(u, NB))
                            sp.wait_ge(S["st_ps"].sem, S["st_ps"].at(u - 2, NP))
                            mv = S[key + "_moved"].sem
                            parts = (0, 1, 0) if name == "q" else (0, 0, 1)
                            if wide:
                                for r, part in enumerate(parts):
                                    row, chunk = (64 * r, 0) if r < 2 else (0, 1)
                                    for j in range(2):
                                        sp.dma_start(T[row:row + 64, half, chunk, j:NH:2, :],
                                                     src[64 * j:64 * j + 64, part, :, :]).then_inc(mv, 16)
                            else:
                                for r, part in enumerate(parts):
                                    sp.dma_start(T[16 * r:16 * r + 16, half, 0, :, :],
                                                 src[:, part, :, :]).then_inc(mv, 16)
                            if mask and name == "k":
                                sp.wait_ge(S["mask_row"].sem, S["mask_row"].at(u, 1))
                                sp.dma_start(KS[MASKROW:MASKROW + 1, half, 0, :, :], MROW[:, :]).then_inc(mv, 16)
                        elif name == "maxT":
                            sp.wait_ge(S["m_hi"].sem, S["m_hi"].at(u, i + 1))
                            sp.wait_ge(S["m_lo"].sem, S["m_lo"].at(u, i + 1))
                            for part in range(2):
                                sp.dma_start(QS[MAXROW + part:MAXROW + part + 1, half, MC,
                                                i * NH // 2:(i + 1) * NH // 2, :],
                                             MH[:, i, part, :]).then_inc(S["m_moved"].sem, 16)

                pipeline(sp, BATCH, body)

            @block.gpsimd
            def _(pool):
                def body(n, c, p):
                    for name, un, i, misc in steps(n, c, p):
                        if name == "stats":
                            u, half = un.u, un.half
                            pool.wait_ge(S["var_ready"].sem, S["var_ready"].at(u, 1))
                            pool.wait_ge(S["xn_ready"].sem, S["xn_ready"].at(u - 2, 1))
                            nc.gpsimd.tensor_tensor(RS[:, half], VE[:, half], g["neghalf"][:, 0:4],
                                                    ALU.pow).then_inc(S["rstd_ready"].sem, 1)

                pipeline(pool, BATCH, body)

            @block.tensor
            def _(pe):
                last = {}

                def previous(p_, c_):
                    for (name, who, i), b in BANK.items():
                        u = {"n": c_.u, "c": p_.u, "p": p_.u - 1}[who]
                        last[b] = release(name, u, i)

                def take(name, who_u, i, key):
                    for sig, u, k in last.get(BANK[key], []):
                        pe.wait_ge(S[sig].sem, S[sig].at(u, k))
                    last[BANK[key]] = release(name, who_u, i)

                def product3(out, pairs, start=True):
                    m = None
                    todo = [(a[x], b[y]) for a, b in pairs for x, y in ((0, 0), (1, 0), (0, 1))]
                    for j, (a, b) in enumerate(todo):
                        m = nc.tensor.matmul(out, a, b, start=(start and j == 0), stop=(j == len(todo) - 1))
                    return m

                def body(n, c, p):
                    if c is not None and p is not None:
                        previous(p, c)
                    for name, un, i, misc in steps(n, c, p):
                        u, half = un.u, un.half
                        key = (name, "n" if un is n else "c" if un is c else "p", i)
                        if name == "xT":
                            pe.wait_ge(S["xn_ready"].sem, S["xn_ready"].at(u, 1))
                            take(name, u, i, key)
                            for kt in range(KT):
                                for t in range(2):
                                    m = nc.tensor.transpose(misc[:, kt * 256 + t * P:kt * 256 + t * P + P],
                                                            XN[:, t, kt * P:kt * P + P], ident[:])
                            m.then_inc(S["xT_ps"].sem, 1)
                        elif name == "cT":
                            if not lnc:
                                pe.wait_ge(S["ctx_in"].sem, S["ctx_in"].at(u, 1))
                            take(name, u, i, key)
                            for kt in range(KT):
                                for t in range(2):
                                    src = CN[:, t, kt * P:kt * P + P] if lnc else CX[:, half, t, kt * P:kt * P + P]
                                    m = nc.tensor.transpose(misc[:, kt * 256 + t * P:kt * 256 + t * P + P],
                                                            src, ident[:])
                            m.then_inc(S["cT_ps"].sem, 1)
                        elif name in ("q", "k"):
                            w, t_, a = (wq, xT, "xT") if name == "q" else (wk, cT, "xT" if self_att else "cT")
                            pe.wait_ge(S[a + "_hi"].sem, S[a + "_hi"].at(u, 1))
                            pe.wait_ge(S[a + "_lo"].sem, S[a + "_lo"].at(u, 1))
                            take(name, u, i, key)
                            for j in range(2):
                                mt = 2 * i + j
                                m = product3(misc[:, j * 256:j * 256 + 256],
                                             [([w[:, x, kt, mt * P:mt * P + P] for x in range(2)],
                                               [t_[:, x, kt, :] for x in range(2)]) for kt in range(KT)])
                            m.then_inc(S[name + "_ps"].sem, 1)
                        elif name == "v":
                            take(name, u, i, key)
                            if NB == 1:
                                for t in range(2):
                                    m = product3(misc[:, t * 256:t * 256 + 256],
                                                 [([cT[:, x, kt, t * P:t * P + P] for x in range(2)],
                                                   [wv[:, x, kt, :] for x in range(2)]) for kt in range(KT)])
                            else:
                                m = product3(misc[:, :],
                                             [([cT[:, x, kt, i * P:i * P + P] for x in range(2)],
                                               [wv[:, x, kt, :] for x in range(2)]) for kt in range(KT)])
                            m.then_inc(S["v_ps"].sem, 1)
                        elif name == "s":
                            if i == 0:
                                pe.wait_ge(S["q_moved"].sem, S["q_moved"].at(u, NQD))
                                pe.wait_ge(S["k_moved"].sem, S["k_moved"].at(u, S["k_moved"].per))
                            take(name, u, i, key)
                            bank = misc
                            for t in range(2):
                                keys = P if causal and t == 0 else SEQ
                                at = (0, P)[t] if causal else t * SEQ
                                for ch, (r0, r1) in enumerate(SR):
                                    m = nc.tensor.matmul(bank[:, at:at + keys],
                                                         QS[r0:r1, half, ch, i, t * P:t * P + P],
                                                         KS[r0:r1, half, ch, i, 0:keys],
                                                         start=(ch == 0), stop=(ch == CH - 1))
                                if causal:
                                    m = nc.tensor.matmul(bank[:, at + keys - P:at + keys], identb[:], g["tri_s"][:],
                                                         start=False, stop=True, skip_group_check=True)
                            m.then_inc(S["s_ps"].sem, 1)
                        elif name == "maxT":
                            pe.wait_ge(S["s_max"].sem, S["s_max"].at(u, (i + 1) * NH // 2))
                            take(name, u, i, key)
                            for t in range(2):
                                m = nc.tensor.transpose(misc[:, t * P:t * P + P], NM[:, i, t, :], ident[:])
                            m.then_inc(S["mT_ps"].sem, 1)
                        elif name == "st":
                            if i % (NH // 2) == 0:
                                pe.wait_ge(S["m_moved"].sem, S["m_moved"].at(u, 2 * (i // (NH // 2)) + 2))
                            if i % 2 == 0:
                                pe.wait_ge(S["p_ready"].sem, S["p_ready"].at(u, i // 2 + 1 - 2))
                            bank = ps[:, 2 + i % 4, :]
                            for t in range(2):
                                q0 = P if causal and t == 1 else 0
                                at = t * SEQ
                                for ch, (r0, r1) in enumerate(TR):
                                    m = nc.tensor.matmul(bank[:, at:at + SEQ - q0],
                                                         KS[r0:r1, half, ch, i, t * P:t * P + P],
                                                         QS[r0:r1, half, ch, i, q0:SEQ],
                                                         start=(ch == 0), stop=(ch == CH - 1))
                                if causal:
                                    m = nc.tensor.matmul(bank[:, at:at + P], identb[:], g["tri_t"][:],
                                                         start=False, stop=True, skip_group_check=True)
                            if i % 2:
                                m.then_inc(S["st_ps"].sem, 1)
                        elif name == "pv":
                            pe.wait_ge(S["p_ready"].sem, S["p_ready"].at(u, (i + 1) * HS // 2))
                            pe.wait_ge(S["v_sb"].sem, S["v_sb"].at(u, NB))
                            pe.wait_ge(S["pv_sb"].sem, S["pv_sb"].at(u, i))
                            for t in range(2):
                                q0 = P if causal and t == 1 else 0
                                for j in range(HS):
                                    h = i * HS + j
                                    rows = slice(0, VW) if wide else slice(32 * j, 32 * j + 32)
                                    at = j * SEQ if wide else 0
                                    if wide and t == 1:
                                        continue
                                    for tt in ((0, 1) if wide else (t,)):
                                        m = nc.tensor.matmul(pvb[rows, at + q0:at + SEQ], VA[:, half, tt, h, :],
                                                             PT[:, h % 8, tt * SEQ:tt * SEQ + SEQ - q0],
                                                             start=(tt == 0), stop=(tt == 1 or causal),
                                                             skip_group_check=bool(causal),
                                                             tile_position=None if wide else (0, 32 * j))
                            m.then_inc(S["pv_ps"].sem, 1)
                        elif name == "oT":
                            pe.wait_ge(S["pv_sb"].sem, S["pv_sb"].at(u, i + 1))
                            take(name, u, i, key)
                            for t in range(2):
                                if wide:
                                    for j in range(HS):
                                        a = (t * HS + j) * W
                                        m = nc.tensor.transpose(misc[:, a:a + VW],
                                                                OS[0:VW, i % 2, j * SEQ + t * P:j * SEQ + t * P + P],
                                                                ident[0:VW, 0:VW])
                                else:
                                    m = nc.tensor.transpose(misc[:, t * P:t * P + P],
                                                            OS[:, i % 2, t * P:t * P + P], ident[:])
                            m.then_inc(S["oT_ps"].sem, 1)
                        elif name == "o2T":
                            pe.wait_ge(S["o_ready"].sem, S["o_ready"].at(u, 4))
                            take(name, u, i, key)
                            for j in range(2):
                                kt = 2 * i + j
                                for t in range(2):
                                    m = nc.tensor.transpose(misc[:, j * 256 + t * P:j * 256 + t * P + P],
                                                            O[:, t, kt * P:kt * P + P], ident[:])
                            m.then_inc(S["o2T_ps"].sem, 1)
                        elif name == "y" and proj:
                            pe.wait_ge(S["o2_hi"].sem, S["o2_hi"].at(u, NB))
                            pe.wait_ge(S["o2_lo"].sem, S["o2_lo"].at(u, NB))
                            take(name, u, i, key)
                            for t in range(2):
                                out = misc[:, t * 256:t * 256 + 256]
                                product3(out, [([oT[:, x, kt, t * P:t * P + P] for x in range(2)],
                                                [wo[:, x, kt, :] for x in range(2)]) for kt in range(CK)])
                                for x in range(2):
                                    m = nc.tensor.matmul(out, g["ones"][0:1, :], brow[0:1, x, :], start=False,
                                                         stop=True, skip_group_check=True)
                            m.then_inc(S["y_ps"].sem, 1)

                pipeline(pe, BATCH, body)

            @block.scalar
            def _(act):
                def body(n, c, p):
                    for name, un, i, misc in steps(n, c, p):
                        u, half = un.u, un.half
                        if name in ("xT", "cT"):
                            dst = xT if name == "xT" else cT
                            act.wait_ge(S[name + "_ps"].sem, S[name + "_ps"].at(u, 1))
                            act.wait_ge(S["v_ps"].sem, S["v_ps"].at(u - 1, NB))
                            nc.scalar.activation(dst[:, 0].rearrange("p k n -> p (k n)"), misc[:, 0:512],
                                                 ACT.Copy).then_inc(S[name + "_hi"].sem, 1)
                        elif name in ("q", "k"):
                            dst, b, hb = (QH, bq, qbias) if name == "q" else (KH, bk, kbias)
                            moved = S[name + "_moved"]
                            fn = ACT.Relu if relu else (ACT.Identity if hb else ACT.Copy)
                            act.wait_ge(moved.sem, moved.at(u - 1, moved.per))
                            sig = S[name + "_hi"]
                            if name == "k" and mask:
                                act.wait_ge(S["k_full"].sem, S["k_full"].at(u, i + 1))
                                nc.scalar.activation(dst[:, 0, 2 * i:2 * i + 2, :], KF[:], ACT.Copy
                                                     ).then_inc(sig.sem, 1)
                                continue
                            act.wait_ge(S[name + "_ps"].sem, S[name + "_ps"].at(u, i + 1))
                            if hb:
                                for j in range(2):
                                    a = nc.scalar.activation(dst[:, 0, 2 * i + j, :],
                                                             misc[:, j * 256:j * 256 + 256], fn,
                                                             bias=b[:, 2 * i + j:2 * i + j + 1])
                            else:
                                a = nc.scalar.activation(dst[:, 0, 2 * i:2 * i + 2, :].rearrange("p k n -> p (k n)"),
                                                         misc[:, :], fn)
                            a.then_inc(sig.sem, 1)
                        elif name == "v":
                            act.wait_ge(S["v_ps"].sem, S["v_ps"].at(u, i + 1))
                            act.wait_ge(S["pv_ps"].sem, S["pv_ps"].at(u - 2, 4))
                            fn = ACT.Relu if relu else ACT.Copy
                            if NB == 1:
                                dst = VA[:, half].rearrange("p t h w -> p (t h) w")[:, :, 0:DH]
                            else:
                                dst = VA[:, half, i, :, 0:DH]
                            nc.scalar.activation(dst, misc[:, :].rearrange("p (h w) -> p h w", w=DH), fn
                                                 ).then_inc(S["v_sb"].sem, 1)
                        elif name == "maxT":
                            act.wait_ge(S["mT_ps"].sem, S["mT_ps"].at(u, i + 1))
                            act.wait_ge(S["m_moved"].sem, S["m_moved"].at(u - 1, 2 * i + 2))
                            nc.scalar.activation(MH[:, i, 0, :], misc[0:NH // 2, 0:SEQ], ACT.Copy
                                                 ).then_inc(S["m_hi"].sem, 1)
                        elif name == "st" and i % 2:
                            act.wait_ge(S["st_ps"].sem, S["st_ps"].at(u, i // 2 + 1))
                            act.wait_ge(S["pv_ps"].sem, S["pv_ps"].at(u, (i - 8) // HS + 1))
                            b0, h0 = 2 + (i - 1) % 4, (i - 1) % 8
                            n_ = SEQ + P if causal else 2 * SEQ
                            nc.scalar.activation(PT[:, h0:h0 + 2, 0:n_], ps[:, b0:b0 + 2, 0:n_],
                                                 ACT.Exp, scale=scale).then_inc(S["p_ready"].sem, 1)
                        elif name == "pv":
                            act.wait_ge(S["pv_ps"].sem, S["pv_ps"].at(u, i + 1))
                            act.wait_ge(S["oT_ps"].sem, S["oT_ps"].at(u, i + 1 - 2))
                            if wide:
                                a = nc.scalar.activation(OS[0:VW, i % 2, :], pvb[0:VW, :], ACT.Copy)
                            else:
                                a = nc.scalar.activation(OS[:, i % 2, 0:SEQ], pvb[:, 0:SEQ], ACT.Copy)
                            a.then_inc(S["pv_sb"].sem, 1)
                        elif name == "o2T":
                            act.wait_ge(S["o2T_ps"].sem, S["o2T_ps"].at(u, i + 1))
                            act.wait_ge(S["y_ps"].sem, S["y_ps"].at(u - 1, 1))
                            nc.scalar.activation(oT[:, 0, 2 * i:2 * i + 2, :].rearrange("p k n -> p (k n)"),
                                                 misc[:, 0:512], ACT.Copy).then_inc(S["o2_hi"].sem, 1)

                pipeline(act, BATCH, body)

            @block.vector
            def _(dve):
                def tiles(T, u):
                    return T[:, bass.ds(u * 2, 2), :]

                def body(n, c, p):
                    for name, un, i, misc in steps(n, c, p):
                        u, half = un.u, un.half
                        if name == "stats":
                            step = S["stats_step"]
                            src = [X[:, bass.ds(u * 2 + t, 1), :] for t in range(2)]
                            if not self_att:
                                dve.wait_ge(S["ctx_in"].sem, S["ctx_in"].at(u, 1))
                            if lnc:
                                src += [CX[:, half, t:t + 1, :] for t in range(2)]
                            nt = len(src)
                            for t, a in enumerate(src):
                                s_ = nc.vector.bn_stats(ST6[:, t, :], a.rearrange("p t d -> p (t d)"))
                            s_.then_inc(step.sem, 1)
                            dve.wait_ge(step.sem, step.at(u, 1))
                            dve.sem_inc(g["S"]["waited"].sem)
                            for t in range(nt):
                                s_ = nc.vector.bn_aggr(MV[:, half, t, :], ST6[:, t, :])
                            s_.then_inc(step.sem, 1)
                            dve.wait_ge(step.sem, step.at(u, 2))
                            dve.wait_ge(S["rstd_ready"].sem, S["rstd_ready"].at(u - 2, 1))
                            v = MV[:, half, 0:2, 1]
                            a1, b1 = (1.0 + EPS, EPS * EPS) if cfg["ln"] == 2 else (1.0, EPS)
                            s_ = nc.vector.tensor_scalar(VE[:, half, 0:2], v, a1, b1, MUL, ADD)
                            if lnc:
                                s_ = nc.vector.tensor_scalar(VE[:, half, 2:4], MV[:, half, 2:4, 1], 1.0, EPS, MUL, ADD)
                            else:
                                s_ = nc.vector.tensor_scalar(VE[:, half, 2:4], v, 1.0, EPS, MUL, ADD)
                            s_.then_inc(S["var_ready"].sem, 1)
                        elif name == "apply":
                            dve.wait_ge(S["rstd_ready"].sem, S["rstd_ready"].at(u, 1))
                            dve.wait_ge(S["xT_ps"].sem, S["xT_ps"].at(u - 1, 1))
                            if lnc:
                                dve.wait_ge(S["cT_ps"].sem, S["cT_ps"].at(u - 1, 1))
                            for t in range(2):
                                xt = X[:, bass.ds(u * 2 + t, 1), :].rearrange("p t d -> p (t d)")
                                s_ = nc.vector.tensor_scalar(XN[:, t, :], xt, MV[:, half, t, 0:1],
                                                             RS[:, half, t:t + 1], SUB, MUL)
                                if self_att:
                                    yt = Y[:, bass.ds(u * 2 + t, 1), :].rearrange("p t d -> p (t d)")
                                    s_ = nc.vector.tensor_scalar(yt, xt, MV[:, half, t, 0:1],
                                                                 RS[:, half, 2 + t:3 + t], SUB, MUL)
                                if lnc:
                                    s_ = nc.vector.tensor_scalar(CN[:, t, :], CX[:, half, t, :],
                                                                 MV[:, half, 2 + t, 0:1],
                                                                 RS[:, half, 2 + t:3 + t], SUB, MUL)
                            s_.then_inc(S["xn_ready"].sem, 1)
                            if mask:
                                dve.wait_ge(S["k_moved"].sem, S["k_moved"].at(u - 1, S["k_moved"].per))
                                dve.wait_ge(S["k_full"].sem, S["k_full"].at(u - 1, 1))
                                nc.vector.tensor_scalar(MKF[:], MKI[:, bass.ds(u * SEQ, SEQ)], 0.0, None, ALU.not_equal)
                                nc.vector.tensor_scalar(MROW[:], MKI[0:NH, bass.ds(u * SEQ, SEQ)], 0.0, -MASKED, ALU.is_equal, MUL
                                                        ).then_inc(S["mask_row"].sem, 1)
                        elif name in ("xT", "cT"):
                            dst = xT if name == "xT" else cT
                            dve.wait_ge(S[name + "_hi"].sem, S[name + "_hi"].at(u, 1))
                            nc.vector.tensor_tensor(dst[:, 1].rearrange("p k n -> p (k n)"), misc[:, 0:512],
                                                    dst[:, 0].rearrange("p k n -> p (k n)"), SUB
                                                    ).then_inc(S[name + "_lo"].sem, 1)
                        elif name in ("q", "k"):
                            dst, b, hb = (QH, bq, qbias) if name == "q" else (KH, bk, kbias)
                            sig = S[name + "_lo"]
                            if name == "k" and mask:
                                dve.wait_ge(S["k_ps"].sem, S["k_ps"].at(u, i + 1))
                                dve.wait_ge(S["mask_row"].sem, S["mask_row"].at(u, 1))
                                dve.wait_ge(S["k_hi"].sem, S["k_hi"].at(u - 1, 1))
                                dve.wait_ge(S["k_lo"].sem, S["k_lo"].at(u - 1, 1))
                                for j in range(2):
                                    s_ = nc.vector.scalar_tensor_tensor(KF[:, j, :], misc[:, j * 256:j * 256 + 256],
                                                                        b[:, 2 * i + j:2 * i + j + 1], MKF[:], ADD, MUL)
                                s_.then_inc(S["k_full"].sem, 1)
                                dve.wait_ge(S["k_hi"].sem, S["k_hi"].at(u, i + 1))
                                nc.vector.tensor_tensor(dst[:, 1, 2 * i:2 * i + 2, :], KF[:],
                                                        dst[:, 0, 2 * i:2 * i + 2, :], SUB).then_inc(sig.sem, 1)
                                continue
                            dve.wait_ge(S[name + "_hi"].sem, S[name + "_hi"].at(u, i + 1))
                            if hb:
                                for j in range(2):
                                    s_ = nc.vector.scalar_tensor_tensor(
                                        dst[:, 1, 2 * i + j, :], misc[:, j * 256:j * 256 + 256],
                                        b[:, 2 * i + j:2 * i + j + 1], dst[:, 0, 2 * i + j, :], ADD, SUB)
                            elif relu:
                                s_ = nc.vector.scalar_tensor_tensor(
                                    dst[:, 1, 2 * i:2 * i + 2, :].rearrange("p k n -> p (k n)"), misc[:, :], 0.0,
                                    dst[:, 0, 2 * i:2 * i + 2, :].rearrange("p k n -> p (k n)"), MAX, SUB)
                            else:
                                s_ = nc.vector.tensor_tensor(
                                    dst[:, 1, 2 * i:2 * i + 2, :].rearrange("p k n -> p (k n)"), misc[:, :],
                                    dst[:, 0, 2 * i:2 * i + 2, :].rearrange("p k n -> p (k n)"), SUB)
                            s_.then_inc(sig.sem, 1)
                        elif name == "s":
                            if i % (NH // 2) == 0:
                                dve.wait_ge(S["mT_ps"].sem, S["mT_ps"].at(u - 1, i // (NH // 2) + 1))
                            dve.wait_ge(S["s_ps"].sem, S["s_ps"].at(u, i + 1))
                            hf, col = i // (NH // 2), i % (NH // 2)
                            if causal:
                                for t, (a, b) in enumerate(((0, P), (P, P + SEQ))):
                                    s_ = nc.vector.tensor_reduce(NM[:, hf, t, col:col + 1], misc[:, a:b],
                                                                 AX.X, MAX, negate=True)
                            else:
                                s_ = nc.vector.tensor_reduce(NM[:, hf, :, col:col + 1],
                                                             misc[:, :].rearrange("p (t k) -> p t k", t=2),
                                                             AX.X, MAX, negate=True)
                            s_.then_inc(S["s_max"].sem, 1)
                        elif name == "maxT":
                            dve.wait_ge(S["m_hi"].sem, S["m_hi"].at(u, i + 1))
                            nc.vector.tensor_tensor(MH[:, i, 1, :], misc[0:NH // 2, 0:SEQ], MH[:, i, 0, :], SUB
                                                    ).then_inc(S["m_lo"].sem, 1)
                        elif name == "oT":
                            dve.wait_ge(S["oT_ps"].sem, S["oT_ps"].at(u, i + 1))
                            nb = 2 * HS
                            view = misc[:, 0:nb * W].rearrange("p (a w) -> p a w", w=W)
                            nc.vector.reciprocal(RC[:, i, 0:nb], view[:, :, DH:DH + 1]).then_inc(S["recip"].sem, 1)
                            dve.wait_ge(S["recip"].sem, S["recip"].at(u, i + 1))
                            if i == 0 and proj:
                                dve.wait_ge(S["o2T_ps"].sem, S["o2T_ps"].at(u - 1, NB))
                            elif i == 0:
                                dve.wait_ge(S["x_done"].sem, S["x_done"].at(u - 1, 1))
                            view4 = misc[:, 0:nb * W].rearrange("p (t a w) -> p t a w", t=2, w=W)[:, :, :, 0:DH]
                            rc = RC[:, i, 0:nb].rearrange("p (t a one) -> p t a one", t=2, one=1).to_broadcast([P, 2, HS, DH])
                            dst = O[:, :, i * HS * DH:(i + 1) * HS * DH].rearrange("p t (a w) -> p t a w", w=DH)
                            nc.vector.tensor_tensor(dst, view4, rc, MUL).then_inc(S["o_ready"].sem, 1)
                        elif name == "o2T":
                            dve.wait_ge(S["o2_hi"].sem, S["o2_hi"].at(u, i + 1))
                            nc.vector.tensor_tensor(oT[:, 1, 2 * i:2 * i + 2, :].rearrange("p k n -> p (k n)"),
                                                    misc[:, 0:512],
                                                    oT[:, 0, 2 * i:2 * i + 2, :].rearrange("p k n -> p (k n)"), SUB
                                                    ).then_inc(S["o2_lo"].sem, 1)
                        elif name == "y":
                            T = Y if self_att else X
                            if proj:
                                dve.wait_ge(S["y_ps"].sem, S["y_ps"].at(u, 1))
                                add = misc[:, :].rearrange("p (t d) -> p t d", t=2)
                            else:
                                dve.wait_ge(S["o_ready"].sem, S["o_ready"].at(u, 4))
                                add = O[:]
                            nc.vector.tensor_tensor(tiles(T, u), add, tiles(T, u), ADD
                                                    ).then_inc(S["x_done"].sem, 1)

                pipeline(dve, BATCH, body)

        for n in ATT + ATT_DMA:
            if signal_used(n, cfg, NB):
                S[n].end(BATCH)


def signal_used(n, cfg, NB):
    proj, mask, self_att = cfg.get("proj"), cfg.get("mask"), cfg.get("self")
    if n in ("o2T_ps", "o2_hi", "o2_lo", "y_ps"):
        return bool(proj)
    if n in ("k_full", "mask_row"):
        return bool(mask)
    if n in ("cT_ps", "cT_hi", "cT_lo", "ctx_in"):
        return not self_att
    return n != "x_step"


def attention_weights(nc, g, S, cfg, wq, wk, wv, wo, bq, bk, brow, C, CK, constants, ones,
                      load_mask):
    proj, relu = cfg.get("proj"), cfg.get("relu")
    w_dram, v_dram, bo_dram = cfg["w"], cfg["vec"], cfg.get("bo")
    setup, loaded = g["setup"], g["loaded"]
    ps = g["ps"]
    with ExitStack() as ctx:
        def sb(name, shape, dt):
            return ctx.enter_context(nc.sbuf_tensor(cfg["name"] + "_" + name, shape, dt))

        WF = sb("WF", [P, 4 if proj else 3, KT * C], F32)
        VEC = sb("VEC", [P, 8 + 3 * CK], F32)
        VB = sb("VB", [P, CK], F32)
        VBB = sb("VBB", [P, CK, P], F32)
        BO = sb("BO", [1, 2, D], F32)
        nw = 4 if proj else 3
        base, lbase = setup.base, loaded.base
        view = [WF[:, n, :].rearrange("p (k c) -> p k c", k=KT) for n in range(3)]
        wof = WF[:, nw - 1, :].rearrange("p (k c) -> p k c", k=CK)
        tabs = [(wq, view[0]), (wk, view[1]), (wv, view[2])] + ([(wo, wof)] if proj else [])
        for n in ("w_sum", "w_hi", "w_lo"):
            S[n].begin(1)
        with nc.Block() as block:
            @block.sync
            def _(sp):
                for n in range(nw):
                    sp.dma_start(WF[:, n, :], w_dram[n]).then_inc(loaded.sem, 16)
                sp.dma_start(VEC[:], v_dram).then_inc(loaded.sem, 16)
                if proj:
                    sp.dma_start(BO[0:1, 0, :], bo_dram).then_inc(loaded.sem, 16)
                if load_mask:
                    load_mask(sp)

            @block.gpsimd
            def _(pool):
                constants(pool)

            @block.scalar
            def _(act):
                act.wait_ge(loaded.sem, lbase + 16 * (nw + (2 if proj else 1)))
                for n, (w, f) in enumerate(tabs):
                    if n < 3:
                        act.wait_ge(S["w_sum"].sem, S["w_sum"].at(n, 1))
                    nc.scalar.activation(w[:, 0], f, ACT.Copy).then_inc(S["w_hi"].sem, 1)

            @block.tensor
            def _(pe):
                pe.wait_ge(loaded.sem, lbase + 16 * (nw + (2 if proj else 1)))
                if proj:
                    for n in range(3):
                        off = 2 if n == 0 else 6
                        for mt in range(CK):
                            for kt in range(KT):
                                m = nc.tensor.matmul(ps[:, 0, 8 * n + mt:8 * n + mt + 1],
                                                     view[n][:, kt, mt * P:mt * P + P], VEC[:, off + kt:off + kt + 1],
                                                     start=(kt == 0), stop=(kt == KT - 1))
                    m.then_inc(setup.sem, 1)
                    pe.wait_ge(setup.sem, base + 3)
                    for kt in range(CK):
                        m = nc.tensor.matmul(ps[:, 1, 0:D], VBB[:, kt, :], wof[:, kt, :],
                                             start=(kt == 0), stop=(kt == CK - 1))
                    m.then_inc(setup.sem, 1)

            @block.vector
            def _(dve):
                dve.wait_ge(loaded.sem, lbase + 16 * (nw + (2 if proj else 1)))
                if proj:
                    dve.wait_ge(setup.sem, base + 1)
                    nc.vector.tensor_tensor(bq[:], ps[:, 0, 0:CK], VEC[:, 8:8 + CK], ADD)
                    nc.vector.tensor_tensor(bk[:], ps[:, 0, 8:8 + CK], VEC[:, 8 + CK:8 + 2 * CK], ADD)
                    nc.vector.tensor_tensor(VB[:], ps[:, 0, 16:16 + CK], VEC[:, 8 + 2 * CK:8 + 3 * CK], ADD
                                            ).then_inc(setup.sem, 1)
                    dve.wait_ge(setup.sem, base + 2)
                    for kt in range(CK):
                        v = nc.vector.tensor_scalar(VBB[:, kt, :], g["onesf"][:, 0:P], VB[:, kt:kt + 1], None, MUL)
                    v.then_inc(setup.sem, 1)
                    dve.wait_ge(setup.sem, base + 4)
                    nc.vector.tensor_tensor(BO[0:1, 1, :], ps[0:1, 1, 0:D], BO[0:1, 0, :], ADD).then_inc(setup.sem, 1)
                    dve.wait_ge(setup.sem, base + 5)
                    nc.vector.tensor_copy(brow[0:1, 0, :], BO[0:1, 1, :]).then_inc(setup.sem, 1)
                    dve.wait_ge(setup.sem, base + 6)
                    nc.vector.tensor_tensor(brow[0:1, 1, :], BO[0:1, 1, :], brow[0:1, 0, :], SUB
                                            ).then_inc(setup.sem, 1)
                    dve.wait_ge(setup.sem, base + 7)
                for n in range(3):
                    off = 0 if n == 0 else 4
                    for kt in range(KT):
                        v = nc.vector.tensor_scalar(view[n][:, kt, :], view[n][:, kt, :],
                                                    VEC[:, off + kt:off + kt + 1], None, MUL)
                    v.then_inc(S["w_sum"].sem, 1)
                for n, (w, f) in enumerate(tabs):
                    dve.wait_ge(S["w_hi"].sem, S["w_hi"].at(n, 1))
                    nc.vector.tensor_tensor(w[:, 1], f, w[:, 0], SUB).then_inc(S["w_lo"].sem, 1)
                dve.wait_ge(S["w_lo"].sem, S["w_lo"].at(nw - 1, 1))
                ones(dve)
        setup.base += 7 if proj else 0
        S["w_sum"].end(3)
        S["w_hi"].end(nw)
        S["w_lo"].end(nw)
        loaded.base += 16 * (nw + (2 if proj else 1))


FFN = ["stats_step", "var_ready", "rstd_ready", "xn_ready", "xT_ps", "xT_hi", "xT_lo", "g_ps", "gate_step", "g_exp",
       "gate_ready", "h_ps", "h_full", "h_hi", "h_lo", "y_ps", "y_half", "y_used", "sel_ps", "sel_sb", "b2_ps", "b2_used"]


def ffn(nc, g, S, cfg):
    E, NE, K = cfg["experts"], cfg["used"], cfg["top"]
    F = cfg["hidden"]
    paired = F < P
    FC = 1 if paired else F // P
    NCH = NE * F // P
    ND = 2 * D if paired else D
    GROUPS = NCH if paired else NE
    UT = 4
    N = UT * P
    UNITS = TOK // N
    RING = 1 if paired else 2
    PARTS = UT if paired else 1
    b1 = cfg.get("b1")
    X, Y, ident = g["X"], g["Y"], g["ident"]
    SRC = Y if cfg.get("from_y") else X
    ps = g["ps"]
    gate_steps = 5 if paired else 10
    for n, s in S.items():
        s.begin(dict(stats_step=2, xT_ps=KT, xT_hi=KT, xT_lo=KT, gate_step=gate_steps, h_ps=NCH, h_full=NCH, h_hi=NCH,
                     h_lo=NCH, y_ps=GROUPS * PARTS, y_half=GROUPS * PARTS,
                     y_used=GROUPS * PARTS).get(n, 1))

    def schedule():
        if paired:
            early = {0: [("stats", 0), ("apply", 0), ("xT", 0)], 1: [("xT", 1)], 2: [("route", 0)],
                     3: [("gate", 0), ("sel", 0), ("b2", 0)]}
        else:
            early = {0: [("stats", 0)], 2: [("apply", 0)], 4: [("xT", 0)], 6: [("xT", 1)], 8: [("route", 0)],
                     10: [("gate", 0)]}
        order = []
        for j in range(NCH):
            order += [("up", "c", j)] + ([("down", "c", j - 1)] if j else [])
            order += [(name, "n", i) for name, i in early.get(j, [])]
        return order + [("down", "c", NCH - 1)]

    ORDER = schedule()

    def steps(n, c):
        for name, who, i in ORDER:
            unit = n if who == "n" else c
            if unit is not None:
                yield name, unit, i

    def pipeline2(eng, body):
        body(Unit(0, 0), None)
        with eng.Fori(0, UNITS // 2 - 1) as i:
            body(Unit(i * 2 + 1, 1), Unit(i * 2, 0))
            body(Unit(i * 2 + 2, 0), Unit(i * 2 + 1, 1))
        body(Unit(UNITS - 1, 1), Unit(UNITS - 2, 0))
        body(None, Unit(UNITS - 1, 1))

    def tile(T, u, t):
        return T[:, bass.ds(u * UT + t, 1), :].rearrange("p t d -> p (t d)")

    with ExitStack() as ctx:
        def sb(name, shape, dt):
            return ctx.enter_context(nc.sbuf_tensor(cfg["name"] + name, shape, dt))

        w1 = sb("w1", [P, 2, KT, NCH * P], BF16)
        w2 = sb("w2", [P, 2, NCH, ND], BF16)
        wg = sb("wg", [P, 2, KT, E], BF16)
        B1 = sb("B1", [P, NCH], F32)
        B2 = sb("B2", [E, D], F32)
        ffn_weights(nc, g, cfg, w1, w2, wg, B1, B2, NCH, ND, E)

        XN = sb("XN", [P, UT, D], F32)
        ST6 = sb("ST6", [P, UT, 6], F32)
        MV = sb("MV", [P, UT, 2], F32)
        VE = sb("VE", [P, UT], F32)
        RS = sb("RS", [P, UT], F32)
        xT = sb("xT", [P, 2, 2, KT, N], BF16)
        HF = sb("HF", [P, 2, N], F32)
        H = sb("H", [P, 2, 2, N], BF16)
        G = sb("G", [P, UT, E], F32)
        M8 = sb("M8", [P, UT, 8], F32)
        GE = sb("GE", [P, UT, E + 8], F32)
        CMP = sb("CMP", [P, UT, NE, E], F32)
        EQ = sb("EQ", [P, UT, NE, E], F32)
        RK = sb("RK", [P, UT, NE], F32)
        SM = sb("SM", [P, UT], F32)
        WT = sb("WT", [P, 2, UT, NE], F32)
        SP_ = sb("SELP", [P, UT, P], F32) if paired else None
        SELT = sb("SELT", [E, N], F32) if paired else None
        setup = g["setup"]
        if paired:
            with nc.Block() as block:
                @block.vector
                def _(dve):
                    nc.vector.memset(SP_[:], 0.0).then_inc(setup.sem, 1)
                    dve.wait_ge(setup.sem, setup.base + 1)
            setup.base += 1

        with nc.Block() as block:
            @block.gpsimd
            def _(pool):
                def body(n, c):
                    for name, un, i in steps(n, c):
                        if name == "stats":
                            pool.wait_ge(S["var_ready"].sem, S["var_ready"].at(un.u, 1))
                            pool.wait_ge(S["xn_ready"].sem, S["xn_ready"].at(un.u - 1, 1))
                            nc.gpsimd.tensor_tensor(RS[:], VE[:], g["neghalf"][:, 0:UT], ALU.pow
                                                    ).then_inc(S["rstd_ready"].sem, 1)

                pipeline2(pool, body)

            @block.tensor
            def _(pe):
                def body(n, c):
                    for name, un, i in steps(n, c):
                        u, half = un.u, un.half
                        if name == "xT":
                            pe.wait_ge(S["xn_ready"].sem, S["xn_ready"].at(u, 1))
                            if paired and i == 0:
                                pe.wait_ge(S["b2_used"].sem, S["b2_used"].at(u - 1, 1))
                            pe.wait_ge(S["xT_hi"].sem, S["xT_hi"].at(u, i))
                            pe.wait_ge(S["xT_lo"].sem, S["xT_lo"].at(u, i))
                            for t in range(UT):
                                m = nc.tensor.transpose(ps[:, 6, t * P:t * P + P], XN[:, t, i * P:i * P + P], ident[:])
                            m.then_inc(S["xT_ps"].sem, 1)
                        elif name == "route":
                            pe.wait_ge(S["xT_hi"].sem, S["xT_hi"].at(u, KT))
                            pe.wait_ge(S["xT_lo"].sem, S["xT_lo"].at(u, KT))
                            pe.wait_ge(S["gate_ready"].sem, S["gate_ready"].at(u - 1, 1))
                            for t in range(UT):
                                todo = [(x, y, kt) for kt in range(KT) for x, y in ((0, 0), (1, 0), (0, 1))]
                                for j, (x, y, kt) in enumerate(todo):
                                    m = nc.tensor.matmul(ps[:, 7, t * E:t * E + E],
                                                         xT[:, half, x, kt, t * P:t * P + P], wg[:, y, kt, :],
                                                         start=(j == 0), stop=(j == len(todo) - 1))
                            m.then_inc(S["g_ps"].sem, 1)
                        elif name == "sel":
                            pe.wait_ge(S["gate_ready"].sem, S["gate_ready"].at(u, 1))
                            for t in range(UT):
                                m = nc.tensor.transpose(ps[:, 6, t * P:t * P + P], SP_[:, t, :], ident[:])
                            m.then_inc(S["sel_ps"].sem, 1)
                        elif name == "b2":
                            pe.wait_ge(S["sel_sb"].sem, S["sel_sb"].at(u, 1))
                            for t in range(UT):
                                m = nc.tensor.matmul(ps[:, 6 + t // 2, (t % 2) * D:(t % 2) * D + D],
                                                     SELT[:, t * P:t * P + P], B2[:], start=True, stop=True)
                            m.then_inc(S["b2_ps"].sem, 1)
                        elif name == "up":
                            if i == 0:
                                pe.wait_ge(S["xT_hi"].sem, S["xT_hi"].at(u, KT))
                                pe.wait_ge(S["xT_lo"].sem, S["xT_lo"].at(u, KT))
                            pe.wait_ge(S["h_hi"].sem, S["h_hi"].at(u, i + 1 - 2))
                            todo = [(x, y, kt) for kt in range(KT) for x, y in ((0, 0), (0, 1), (1, 0))]
                            for j, (x, y, kt) in enumerate(todo):
                                m = nc.tensor.matmul(ps[:, i % 2, :], w1[:, x, kt, i * P:i * P + P],
                                                     xT[:, half, y, kt, :], start=(j == 0), stop=(j == len(todo) - 1))
                            m.then_inc(S["h_ps"].sem, 1)
                        elif name == "down":
                            e, f = i // FC, i % FC
                            pe.wait_ge(S["h_lo"].sem, S["h_lo"].at(u, i + 1))
                            if f == 0 and not paired:
                                pe.wait_ge(S["y_used"].sem, S["y_used"].at(u, e + 1 - RING))
                            for t in range(UT):
                                if paired:
                                    pe.wait_ge(S["y_used"].sem, S["y_used"].at(u, (e - 1) * UT + t + 1))
                                    out = ps[:, 2 + t, :]
                                else:
                                    out = ps[:, 2 + 2 * (e % 2) + t // 2, (t % 2) * D:(t % 2) * D + D]
                                for j, (x, y) in enumerate(((0, 0), (0, 1), (1, 0))):
                                    first = f == 0 and j == 0 and (paired or t % 2 == 0)
                                    m = nc.tensor.matmul(out, H[:, i % 2, x, t * P:t * P + P], w2[:, y, i, :],
                                                         start=first, stop=(f == FC - 1 and j == 2),
                                                         skip_group_check=not paired)
                                if paired:
                                    m.then_inc(S["y_ps"].sem, 1)
                            if f == FC - 1 and not paired:
                                m.then_inc(S["y_ps"].sem, 1)

                pipeline2(pe, body)

            @block.scalar
            def _(act):
                def body(n, c):
                    for name, un, i in steps(n, c):
                        u, half = un.u, un.half
                        if name == "xT":
                            act.wait_ge(S["xT_ps"].sem, S["xT_ps"].at(u, i + 1))
                            act.wait_ge(S["h_ps"].sem, S["h_ps"].at(u - 2, NCH))
                            nc.scalar.activation(xT[:, half, 0, i, :], ps[:, 6, :], ACT.Copy
                                                 ).then_inc(S["xT_hi"].sem, 1)
                        elif name == "gate" and not paired:
                            act.wait_ge(S["gate_step"].sem, S["gate_step"].at(u, 3))
                            nc.scalar.activation(GE[:], GE[:], ACT.Exp).then_inc(S["g_exp"].sem, 1)
                        elif name == "sel":
                            act.wait_ge(S["sel_ps"].sem, S["sel_ps"].at(u, 1))
                            nc.scalar.activation(SELT[:], ps[0:E, 6, :], ACT.Copy).then_inc(S["sel_sb"].sem, 1)
                        elif name == "up":
                            act.wait_ge(S["h_ps"].sem, S["h_ps"].at(u, i + 1))
                            act.wait_ge(S["h_lo"].sem, S["h_lo"].at(u, i + 1 - 2))
                            bias = {"bias": B1[:, i:i + 1]} if b1 else {}
                            nc.scalar.activation(HF[:, i % 2, :], ps[:, i % 2, :], cfg["gelu"], **bias
                                                 ).then_inc(S["h_full"].sem, 1)
                            nc.scalar.activation(H[:, i % 2, 0, :], ps[:, i % 2, :], cfg["gelu"], **bias
                                                 ).then_inc(S["h_hi"].sem, 1)

                pipeline2(act, body)

            @block.vector
            def _(dve):
                def combine(u, half, e):
                    if e == 0:
                        dve.wait_ge(S["gate_ready"].sem, S["gate_ready"].at(u, 1))
                        if paired or cfg.get("from_y"):
                            dve.wait_ge(S["b2_used"].sem, S["b2_used"].at(u, 1))
                    if not paired:
                        dve.wait_ge(S["y_ps"].sem, S["y_ps"].at(u, e + 1))
                        dve.wait_ge(S["y_used"].sem, S["y_used"].at(u, e))
                        for t in range(UT):
                            y = ps[:, 2 + 2 * (e % 2) + t // 2, (t % 2) * D:(t % 2) * D + D]
                            v = nc.vector.scalar_tensor_tensor(tile(X, u, t), y, WT[:, half, t, e:e + 1],
                                                               tile(X, u, t), MUL, ADD)
                        v.then_inc(S["y_used"].sem, 1)
                        return
                    for t in range(UT + 1):
                        if t < UT:
                            done = e * UT + t
                            dve.wait_ge(S["y_ps"].sem, S["y_ps"].at(u, done + 1))
                            dve.wait_ge(S["y_used"].sem, S["y_used"].at(u, done + 1 - UT))
                            nc.vector.scalar_tensor_tensor(tile(X, u, t), ps[:, 2 + t, 0:D],
                                                           WT[:, half, t, 2 * e:2 * e + 1], tile(X, u, t),
                                                           MUL, ADD).then_inc(S["y_half"].sem, 1)
                        if t:
                            dve.wait_ge(S["y_half"].sem, S["y_half"].at(u, e * UT + t))
                            nc.vector.scalar_tensor_tensor(tile(X, u, t - 1), ps[:, 1 + t, D:2 * D],
                                                           WT[:, half, t - 1, 2 * e + 1:2 * e + 2],
                                                           tile(X, u, t - 1), MUL, ADD
                                                           ).then_inc(S["y_used"].sem, 1)

                def gate(u, half):
                    step, k = S["gate_step"], 0

                    def link(ins):
                        nonlocal k
                        k += 1
                        ins.then_inc(step.sem, 1)
                        dve.wait_ge(step.sem, step.at(u, k))

                    dve.wait_ge(S["g_ps"].sem, S["g_ps"].at(u, 1))
                    link(nc.vector.tensor_copy(G[:].rearrange("p t e -> p (t e)"), ps[:, 7, 0:UT * E]))
                    if not paired:
                        dve.sem_inc(S["waited"].sem)
                        for t in range(UT):
                            v = nc.vector.max(M8[:, t, :], G[:, t, :])
                        link(v)
                        top = M8[:, :, 0:1]
                        nc.vector.tensor_tensor(GE[:, :, 0:E], G[:], top.to_broadcast([P, UT, E]), SUB)
                        link(nc.vector.tensor_tensor(GE[:, :, E:E + 8], M8[:], top.to_broadcast([P, UT, 8]), SUB))
                    every = G[:].rearrange("p t (one e) -> p t one e", one=1).to_broadcast([P, UT, NE, E])
                    own = G[:, :, 0:NE].rearrange("p t (e one) -> p t e one", one=1).to_broadcast([P, UT, NE, E])
                    nc.vector.tensor_tensor(CMP[:], every, own, ALU.is_gt)
                    link(nc.vector.tensor_tensor(EQ[:], every, own, ALU.is_equal))
                    for t in range(UT):
                        v = nc.vector.tensor_tensor(EQ[:, t], EQ[:, t], g["tri"][:, 0:NE, 0:E], MUL)
                    link(v)
                    link(nc.vector.tensor_tensor(CMP[:], CMP[:], EQ[:], ADD))
                    link(nc.vector.tensor_reduce(RK[:], CMP[:], AX.X, ADD))
                    if paired:
                        dve.wait_ge(S["sel_ps"].sem, S["sel_ps"].at(u - 1, 1))
                        nc.vector.tensor_scalar(WT[:, half], RK[:], float(K), None, ALU.is_lt)
                        nc.vector.tensor_scalar(SP_[:, :, 0:NE], RK[:], float(K), None, ALU.is_lt
                                                ).then_inc(S["gate_ready"].sem, 1)
                        return
                    dve.wait_ge(S["g_exp"].sem, S["g_exp"].at(u, 1))
                    link(nc.vector.tensor_reduce(SM[:], GE[:, :, E:E + K], AX.X, ADD))
                    link(nc.vector.reciprocal(SM[:], SM[:]))
                    link(nc.vector.scalar_tensor_tensor(WT[:, half], RK[:], float(K), GE[:, :, 0:NE], ALU.is_lt, MUL))
                    nc.vector.tensor_tensor(WT[:, half], WT[:, half],
                                            SM[:].rearrange("p (t one) -> p t one", one=1).to_broadcast([P, UT, NE]),
                                            MUL).then_inc(S["gate_ready"].sem, 1)

                def body(n, c):
                    for name, un, i in steps(n, c):
                        u, half = un.u, un.half
                        if name == "stats":
                            step = S["stats_step"]
                            for t in range(UT):
                                v = nc.vector.bn_stats(ST6[:, t, :], tile(SRC, u, t))
                            v.then_inc(step.sem, 1)
                            dve.wait_ge(step.sem, step.at(u, 1))
                            dve.sem_inc(g["S"]["waited"].sem)
                            for t in range(UT):
                                v = nc.vector.bn_aggr(MV[:, t, :], ST6[:, t, :])
                            v.then_inc(step.sem, 1)
                            dve.wait_ge(step.sem, step.at(u, 2))
                            dve.wait_ge(S["rstd_ready"].sem, S["rstd_ready"].at(u - 1, 1))
                            a, b = (1.0 + EPS, EPS * EPS) if cfg["ln"] == 2 else (1.0, EPS)
                            nc.vector.tensor_scalar(VE[:], MV[:, :, 1], a, b, MUL, ADD
                                                    ).then_inc(S["var_ready"].sem, 1)
                        elif name == "apply":
                            dve.wait_ge(S["rstd_ready"].sem, S["rstd_ready"].at(u, 1))
                            dve.wait_ge(S["xT_ps"].sem, S["xT_ps"].at(u - 1, KT))
                            for t in range(UT):
                                v = nc.vector.tensor_scalar(XN[:, t, :], tile(SRC, u, t), MV[:, t, 0:1],
                                                            RS[:, t:t + 1], SUB, MUL)
                            v.then_inc(S["xn_ready"].sem, 1)
                            if cfg.get("from_y"):
                                for t in range(UT):
                                    v = nc.vector.tensor_tensor(tile(X, u, t), tile(X, u, t), tile(Y, u, t), ADD)
                                v.then_inc(S["b2_used"].sem, 1)
                        elif name == "xT":
                            dve.wait_ge(S["xT_hi"].sem, S["xT_hi"].at(u, i + 1))
                            nc.vector.tensor_tensor(xT[:, half, 1, i, :], ps[:, 6, :], xT[:, half, 0, i, :], SUB
                                                    ).then_inc(S["xT_lo"].sem, 1)
                        elif name == "gate":
                            gate(u, half)
                        elif name == "b2":
                            dve.wait_ge(S["b2_ps"].sem, S["b2_ps"].at(u, 1))
                            for t in range(UT):
                                v = nc.vector.tensor_tensor(tile(X, u, t), ps[:, 6 + t // 2, (t % 2) * D:(t % 2) * D + D],
                                                            tile(X, u, t), ADD)
                            v.then_inc(S["b2_used"].sem, 1)
                        elif name == "up":
                            dve.wait_ge(S["h_hi"].sem, S["h_hi"].at(u, i + 1))
                            nc.vector.tensor_tensor(H[:, i % 2, 1, :], HF[:, i % 2, :], H[:, i % 2, 0, :], SUB
                                                    ).then_inc(S["h_lo"].sem, 1)
                        elif name == "down" and i % FC == FC - 1:
                            combine(u, half, i // FC)

                pipeline2(dve, body)

        for n in FFN:
            if n in ("sel_ps", "sel_sb", "b2_ps", "y_half") and not paired:
                continue
            if n == "b2_used" and not (paired or cfg.get("from_y")):
                continue
            if n == "g_exp" and paired:
                continue
            S[n].end(UNITS)


def ffn_weights(nc, g, cfg, w1, w2, wg, B1, B2, NCH, ND, E):
    S = g["S"]
    ps, loaded, setup = g["ps"], g["loaded"], g["setup"]
    lora, gamma, paired = cfg.get("lora"), cfg.get("gamma"), ND > D
    PIECE = 4 * D
    n1, n2 = KT * NCH * P // PIECE, NCH * ND // PIECE
    pieces = [("w1", n) for n in range(n1)] + [("w2", n) for n in range(n2)]
    per_kt = n1 // KT
    names = ("w_ps", "w_sum", "w_hi", "w_lo")
    for n in names:
        S[n].begin(1)
    RING = 4
    with ExitStack() as ctx:
        def sb(name, shape, dt):
            return ctx.enter_context(nc.sbuf_tensor(cfg["name"] + "_" + name, shape, dt))

        WF = sb("WF", [P, RING, PIECE], F32)
        WG = sb("WG", [P, KT, E], F32)
        GA = sb("GA", [P, KT * (E if paired else 1)], F32) if gamma is not None else None
        BE = sb("BE", [P, KT * E], F32) if paired else None
        BI = sb("BI", [P, NCH], F32) if paired else None
        LO = {n: sb("L" + n, [a.shape[0], a.shape[1]], F32) for n, a in lora.items()} if lora else {}
        base, lbase = setup.base, loaded.base
        small = [(WG[:].rearrange("p k e -> p (k e)"), cfg["wg"])]
        if gamma is not None:
            small.append((GA[:], gamma))
        if paired:
            small += [(BE[:], cfg["beta"]), (BI[:], cfg["b1"]), (B2[:], cfg["b2"])]
        if lora:
            small += [(LO[n][:], a) for n, a in lora.items()]
        all_small = lbase + 16 * len(small)
        def w_in(j):
            s = S["w_in%d" % (j % RING)]
            return s.sem, s.base + 16 * (j // RING + 1)

        dst = {"w1": w1[:].rearrange("p x k c -> p x (k c)"), "w2": w2[:].rearrange("p x k c -> p x (k c)")}

        with nc.Block() as block:
            @block.sync
            def _(sp):
                for t, a in small:
                    sp.dma_start(t, a).then_inc(loaded.sem, 16)
                for j, (w, n) in enumerate(pieces):
                    sp.wait_ge(S["w_lo"].sem, S["w_lo"].at(j - RING, 1))
                    sp.dma_start(WF[:, j % RING, :], cfg[w][:, n * PIECE:(n + 1) * PIECE]).then_inc(w_in(j)[0], 16)

            @block.tensor
            def _(pe):
                pe.wait_ge(loaded.sem, all_small)
                if paired:
                    pe.wait_ge(*w_in(0))
                    raw = WF[:, 0, :].rearrange("p (k c) -> p k c", k=KT)
                    be = BE[:].rearrange("p (k e) -> p k e", k=KT)
                    H_ = P // 2
                    for e in range(E):
                        rows = slice(H_ * (e % 2), H_ * (e % 2) + H_)
                        for kt in range(KT):
                            m = nc.tensor.matmul(ps[rows, 0, e // 2:e // 2 + 1], raw[:, kt, e * H_:(e + 1) * H_],
                                                 be[:, kt, e:e + 1], start=(kt == 0), stop=(kt == KT - 1),
                                                 tile_position=(0, H_ * (e % 2)))
                    m.then_inc(setup.sem, 1)
                if lora:
                    for j, (w, n) in enumerate(pieces):
                        pe.wait_ge(S["w_sum"].sem, S["w_sum"].at(j - 2, 1))
                        if w == "w1":
                            kt, e = n // per_kt, n % per_kt
                            for c in range(2):
                                m = nc.tensor.matmul(ps[:, 2 * (j % 2) + c, :],
                                                     LO["a1"][:, e * D + kt * P:e * D + kt * P + P],
                                                     LO["b1"][:, e * 1024 + c * 512:e * 1024 + c * 512 + 512],
                                                     start=True, stop=True)
                        else:
                            e = n // 2
                            for c in range(4):
                                f = 4 * n + c
                                m = nc.tensor.matmul(ps[:, 2 * (j % 2) + c // 2, (c % 2) * D:(c % 2) * D + D],
                                                     LO["a2"][:, f * P:f * P + P], LO["b2"][:, e * D:(e + 1) * D],
                                                     start=True, stop=True)
                        m.then_inc(S["w_ps"].sem, 1)

            @block.scalar
            def _(act):
                for j, (w, n) in enumerate(pieces):
                    act.wait_ge(S["w_sum"].sem, S["w_sum"].at(j, 1))
                    nc.scalar.activation(dst[w][:, 0, n * PIECE:(n + 1) * PIECE], WF[:, j % RING, :], ACT.Copy
                                         ).then_inc(S["w_hi"].sem, 1)

            @block.vector
            def _(dve):
                dve.wait_ge(loaded.sem, all_small)
                ga = GA[:].rearrange("p (k e) -> p k e", k=KT) if gamma is not None else None
                if gamma is not None and not paired:
                    for kt in range(KT):
                        v = nc.vector.tensor_scalar(WG[:, kt], WG[:, kt], ga[:, kt, 0:1], None, MUL)
                else:
                    v = nc.vector.tensor_scalar(WG[:], WG[:], 1.0, None, MUL)
                if paired:
                    dve.wait_ge(setup.sem, base + 1)
                v.then_inc(setup.sem, 1) if not paired else None
                if paired:
                    nc.vector.tensor_tensor(B1[:], ps[:, 0, 0:NCH], BI[:], ADD).then_inc(setup.sem, 1)
                n_ = base + (2 if paired else 1)
                dve.wait_ge(setup.sem, n_)
                nc.vector.tensor_copy(wg[:, 0], WG[:]).then_inc(setup.sem, 1)
                dve.wait_ge(setup.sem, n_ + 1)
                nc.vector.tensor_tensor(wg[:, 1], WG[:], wg[:, 0], SUB).then_inc(setup.sem, 1)

                def split(j, w, n):
                    dve.wait_ge(S["w_hi"].sem, S["w_hi"].at(j, 1))
                    nc.vector.tensor_tensor(dst[w][:, 1, n * PIECE:(n + 1) * PIECE], WF[:, j % RING, :],
                                            dst[w][:, 0, n * PIECE:(n + 1) * PIECE], SUB).then_inc(S["w_lo"].sem, 1)

                for j, (w, n) in enumerate(pieces):
                    f = WF[:, j % RING, :]
                    dve.wait_ge(*w_in(j))
                    if lora:
                        dve.wait_ge(S["w_ps"].sem, S["w_ps"].at(j, 1))
                        low_rank = ps[:, 2 * (j % 2):2 * (j % 2) + 2, :].rearrange("p a n -> p (a n)")
                        v = nc.vector.tensor_tensor(f, low_rank, f, ADD)
                    elif paired and w == "w1":
                        for kt in range(KT):
                            fk = f.rearrange("p (k e h) -> p k e h", k=KT, e=E)[:, kt]
                            gk = ga[:, kt, :].rearrange("p (e one) -> p e one", one=1).to_broadcast([P, E, P // 2])
                            v = nc.vector.tensor_tensor(fk, fk, gk, MUL)
                    elif gamma is not None and w == "w1":
                        v = nc.vector.tensor_scalar(f, f, ga[:, n // per_kt, 0:1], None, MUL)
                    else:
                        v = nc.vector.tensor_scalar(f, f, 1.0, None, MUL)
                    v.then_inc(S["w_sum"].sem, 1)
                    if j:
                        split(j - 1, *pieces[j - 1])
                split(len(pieces) - 1, *pieces[-1])

        setup.base += 4 if paired else 3
        loaded.base += 16 * len(small)
        for n in names:
            if n != "w_ps" or lora:
                S[n].end(len(pieces))
        for r in range(RING):
            S["w_in%d" % r].base += 16 * len(range(r, len(pieces), RING))


FP8_MAX = 448.0
TO_FP8 = 1.5 * 2.0 ** 20
FP8_LEAST = 2.0 ** -6
Q8 = ["stats_step", "var_ready", "rstd_ready", "n_ready", "quant_step", "q8_ready", "q8T_ps", "q8T_sb", "acc_ps",
      "acc_bf", "out_ready"]


def quantised_linear(nc, g, S, w_dram, bias_dram, out_rows):
    X, Y, ps = g["X"], g["Y"], g["ps"]
    UT = 4
    UNITS = TILES // UT
    for n in Q8 + ["out_done0", "out_done1"]:
        S[n].begin({"stats_step": 3, "quant_step": 4}.get(n, 1))
    setup, loaded = g["setup"], g["loaded"]

    def rows(T, u):
        return T[:, bass.ds(u * UT, UT), :]

    def tile(T, u, t):
        return T[:, bass.ds(u * UT + t, 1), :].rearrange("p t d -> p (t d)")

    with ExitStack() as ctx:
        def sb(name, shape, dt):
            return ctx.enter_context(nc.sbuf_tensor("q8" + name, shape, dt))

        WF = sb("WF", [P, KT * D], F32)
        BI = sb("BI", [P, D], F32)
        ST6 = sb("ST6", [P, UT, 6], F32)
        MV = sb("MV", [P, UT, 2], F32)
        VE = sb("VE", [P, UT], F32)
        RS = sb("RS", [P, UT], F32)
        AM = sb("AM", [P, UNITS], F32)
        A2 = sb("A2", [P, 2], F32)
        AR = sb("AR", [P, 2], F32)
        SC = sb("SC", [P, 2], F32)
        IS = sb("IS", [P, 3], F32)
        WQ = sb("WQ", [P, KT * D], BF16)
        T1 = sb("T1", [P, UT * D], F32)
        T2 = sb("T2", [P, UT * D], F32)
        Q = sb("Q", [P, UT * D], BF16)
        QT = sb("QT", [P, 2, KT * UT * P], BF16)
        OB = sb("OB", [P, UT * D], BF16)
        OUT = sb("OUT", [P, 2, UT, D], F32)

        lb = loaded.base
        with nc.Block() as block:
            @block.sync
            def _(sp):
                sp.dma_start(WF[:], w_dram).then_inc(loaded.sem, 16)
                sp.dma_start(BI[:], bias_dram.to_broadcast([P, D])).then_inc(loaded.sem, 16)
                sp.wait_ge(loaded.sem, lb + 32)

            @block.gpsimd
            def _(pool):
                with pool.Fori(0, UNITS) as u:
                    pool.wait_ge(S["var_ready"].sem, S["var_ready"].at(u, 1))
                    nc.gpsimd.tensor_tensor(RS[:], VE[:], g["neghalf"][:, 0:UT], ALU.pow
                                            ).then_inc(S["rstd_ready"].sem, 1)

            @block.vector
            def _(dve):
                step = S["stats_step"]
                with dve.Fori(0, UNITS) as u:
                    for t in range(UT):
                        v = nc.vector.bn_stats(ST6[:, t, :], tile(X, u, t))
                    v.then_inc(step.sem, 1)
                    dve.wait_ge(step.sem, step.at(u, 1))
                    dve.sem_inc(g["S"]["waited"].sem)
                    for t in range(UT):
                        v = nc.vector.bn_aggr(MV[:, t, :], ST6[:, t, :])
                    v.then_inc(step.sem, 1)
                    dve.wait_ge(step.sem, step.at(u, 2))
                    nc.vector.tensor_scalar(VE[:], MV[:, :, 1], 1.0, EPS, MUL, ADD).then_inc(S["var_ready"].sem, 1)
                    dve.wait_ge(S["rstd_ready"].sem, S["rstd_ready"].at(u, 1))
                    for t in range(UT):
                        v = nc.vector.tensor_scalar(tile(Y, u, t), tile(X, u, t), MV[:, t, 0:1], RS[:, t:t + 1],
                                                    SUB, MUL)
                    v.then_inc(step.sem, 1)
                    dve.wait_ge(step.sem, step.at(u, 3))
                    nc.vector.tensor_reduce(AM[:, bass.ds(u, 1)], rows(Y, u).rearrange("p t d -> p (t d)"), AX.X, MAX,
                                            apply_absolute_value=True).then_inc(S["n_ready"].sem, 1)

        loaded.base += 32
        for n in ("stats_step", "var_ready", "rstd_ready", "n_ready"):
            S[n].end(UNITS)

        def quantise(dve, dst, src, scale, link):
            link(nc.vector.tensor_scalar(T1[:, 0:src.shape[1]], src, scale, FP8_MAX, MUL, MIN))
            n = src.shape[1]
            t1, t2 = T1[:, 0:n], T2[:, 0:n]
            link(nc.vector.tensor_scalar(t2.bitcast(I32), t1.bitcast(I32), 0x7F800000, None, ALU.bitwise_and))
            link(nc.vector.tensor_scalar(t2, t2, FP8_LEAST, TO_FP8, MAX, MUL))
            link(nc.vector.scalar_tensor_tensor(t1, t1, -FP8_MAX, t2, MAX, ADD))
            return nc.vector.tensor_tensor(dst, t1, t2, SUB)

        base = setup.base
        with nc.Block() as block:
            @block.gpsimd
            def _(pool):
                pool.wait_ge(setup.sem, base + 2)
                nc.gpsimd.partition_all_reduce(AR[:], A2[:], P, bass.bass_isa.ReduceOp.max).then_inc(setup.sem, 1)

            @block.vector
            def _(dve):
                seen = [base]

                def link(ins):
                    seen[0] += 1
                    ins.then_inc(setup.sem, 1)
                    dve.wait_ge(setup.sem, seen[0])

                link(nc.vector.tensor_reduce(A2[:, 0:1], AM[:], AX.X, MAX))
                link(nc.vector.tensor_reduce(A2[:, 1:2], WF[:], AX.X, MAX, apply_absolute_value=True))
                seen[0] += 1
                dve.wait_ge(setup.sem, seen[0])
                link(nc.vector.tensor_scalar(AR[:], AR[:], 1e-12, None, MAX))
                link(nc.vector.reciprocal(SC[:], AR[:]))
                link(nc.vector.tensor_scalar(SC[:], SC[:], FP8_MAX, FP8_MAX, MUL, MIN))
                link(nc.vector.reciprocal(IS[:, 0:2], SC[:]))
                link(nc.vector.tensor_tensor(IS[:, 2:3], IS[:, 0:1], IS[:, 1:2], MUL))
                link(quantise(dve, WQ[:], WF[:], SC[:, 1:2], link))

        setup.base += 13
        with nc.Block() as block:
            def pipeline1(eng, body):
                body(0, 0, None, 0, 0)
                with eng.Fori(0, UNITS // 2 - 1) as i:
                    body(i * 2 + 1, 1, i * 2, 0, i)
                    body(i * 2 + 2, 0, i * 2 + 1, 1, i)
                body(UNITS - 1, 1, UNITS - 2, 0, UNITS // 2 - 1)
                body(None, 0, UNITS - 1, 1, UNITS // 2 - 1)

            @block.vector
            def _(dve):
                def body(n, nh, c, ch, pair):
                    if n is not None:
                        k = [0]

                        def link(ins):
                            k[0] += 1
                            ins.then_inc(S["quant_step"].sem, 1)
                            dve.wait_ge(S["quant_step"].sem, S["quant_step"].at(n, k[0]))

                        dve.wait_ge(S["q8T_ps"].sem, S["q8T_ps"].at(n - 1, 1))
                        quantise(dve, Q[:], rows(Y, n).rearrange("p t d -> p (t d)"), SC[:, 0:1], link
                                 ).then_inc(S["q8_ready"].sem, 1)
                    if c is not None:
                        dve.wait_ge(S["acc_ps"].sem, S["acc_ps"].at(c, 1))
                        dve.wait_ge(S["out_ready"].sem, S["out_ready"].at(c - 1, 1))
                        for t in range(UT):
                            acc = ps[:, 2 * ch + t // 2, (t % 2) * D:(t % 2) * D + D]
                            v = nc.vector.scalar_tensor_tensor(OB[:, t * D:t * D + D], acc, IS[:, 2:3], BI[:],
                                                               MUL, ADD)
                        v.then_inc(S["acc_bf"].sem, 1)
                        dve.wait_ge(S["acc_bf"].sem, S["acc_bf"].at(c, 1))
                        dve.wait_ge(S["out_done%d" % ch].sem, S["out_done%d" % ch].at(pair - 1, 1))
                        nc.vector.tensor_tensor(OUT[:, ch].rearrange("p t d -> p (t d)"),
                                                rows(X, c).rearrange("p t d -> p (t d)"), OB[:], ADD
                                                ).then_inc(S["out_ready"].sem, 1)

                pipeline1(dve, body)

            @block.tensor
            def _(pe):
                def body(n, nh, c, ch, pair):
                    if n is not None:
                        pe.wait_ge(S["q8_ready"].sem, S["q8_ready"].at(n, 1))
                        pe.wait_ge(S["q8T_sb"].sem, S["q8T_sb"].at(n - 1, 1))
                        tp = ps[:, 6, :].bitcast(BF16)
                        for kt in range(KT):
                            for t in range(UT):
                                m = nc.tensor.transpose(tp[:, (kt * UT + t) * P:(kt * UT + t) * P + P],
                                                        Q[:, t * D + kt * P:t * D + kt * P + P], g["identb"][:])
                        m.then_inc(S["q8T_ps"].sem, 1)
                    if c is not None:
                        pe.wait_ge(S["q8T_sb"].sem, S["q8T_sb"].at(c, 1))
                        pe.wait_ge(S["acc_bf"].sem, S["acc_bf"].at(c - 2, 1))
                        for t in range(UT):
                            for kt in range(KT):
                                m = nc.tensor.matmul(ps[:, 2 * ch + t // 2, (t % 2) * D:(t % 2) * D + D],
                                                     QT[:, ch, (kt * UT + t) * P:(kt * UT + t) * P + P],
                                                     WQ[:, kt * D:kt * D + D], start=(kt == 0), stop=(kt == KT - 1))
                        m.then_inc(S["acc_ps"].sem, 1)

                pipeline1(pe, body)

            @block.scalar
            def _(act):
                def body(n, nh, c, ch, pair):
                    if n is not None:
                        act.wait_ge(S["q8T_ps"].sem, S["q8T_ps"].at(n, 1))
                        act.wait_ge(S["acc_ps"].sem, S["acc_ps"].at(n - 2, 1))
                        nc.scalar.activation(QT[:, nh, :], ps[:, 6, :].bitcast(BF16), ACT.Copy
                                             ).then_inc(S["q8T_sb"].sem, 1)

                pipeline1(act, body)

            @block.sync
            def _(sp):
                def body(n, nh, c, ch, pair):
                    if c is not None:
                        sp.wait_ge(S["out_ready"].sem, S["out_ready"].at(c, 1))
                        dst = out_rows[bass.ds(c * UT, UT), :, :].rearrange("t p d -> p t d")
                        sp.dma_start(dst, OUT[:, ch]).then_inc(S["out_done%d" % ch].sem, 16)

                pipeline1(sp, body)
                for n in ("out_done0", "out_done1"):
                    sp.wait_ge(S[n].sem, S[n].at(UNITS // 2 - 1, 1))


def network(nc, t, out):
    with ExitStack() as ctx:
        def sb(name, shape, dt):
            return ctx.enter_context(nc.sbuf_tensor(name, shape, dt))

        names = list(dict.fromkeys(ATT + FFN + Q8 + ["w_ps", "w_sum", "w_hi", "w_lo", "setup", "const_ready", "waited"]))
        S = signals(ctx, nc, names, ATT_DMA + ["w_in0", "w_in1", "w_in2", "w_in3", "loaded", "mask_in", "out_done0", "out_done1"])
        g = {"S": S, "setup": S["setup"], "loaded": S["loaded"]}
        g["X"] = sb("X", [P, TILES, D], F32)
        g["Y"] = sb("Y", [P, TILES, D], F32)
        g["ident"] = sb("ident", [P, P], F32)
        g["identb"] = sb("identb", [P, P], BF16)
        g["ones"] = sb("ones", [P, P], BF16)
        g["onesf"] = sb("onesf", [P, P], F32)
        g["neghalf"] = sb("neghalf", [P, 8], F32)
        g["tri_s"] = sb("tri_s", [P, P], BF16)
        g["tri_t"] = sb("tri_t", [P, P], BF16)
        g["tri"] = sb("tri", [P, 16, 16], F32)
        g["ps"] = ctx.enter_context(nc.psum_tensor("ps", [P, 8, 512], F32))
        g["ctx_rows"] = t["ctx"].rearrange("(t p) d -> t p d", p=P)
        g["mask"] = t["mask"]
        x_rows = t["x"].rearrange("(t p) d -> p t d", p=P)
        setup, loaded = S["setup"], S["loaded"]

        with nc.Block() as block:
            @block.sync
            def _(sp):
                for s in S.values():
                    sp.sem_inc(s.sem, Signal.START)

        base = setup.base
        with nc.Block() as block:
            @block.sync
            def _(sp):
                sp.dma_start(g["X"][:], x_rows).then_inc(loaded.sem, 16)
                sp.wait_ge(loaded.sem, loaded.base + 16)

            @block.gpsimd
            def _(pool):
                for n, v in (("ident", 0.0), ("identb", 0.0), ("ones", 1.0), ("onesf", 1.0), ("neghalf", -0.5),
                             ("tri_s", 0.0), ("tri_t", 0.0), ("tri", 1.0)):
                    nc.gpsimd.memset(g[n][:], v).then_inc(setup.sem, 1)
                pool.wait_ge(setup.sem, base + 8)
                for n in ("ident", "identb"):
                    pool.affine_select(out=g[n][:], in_=g[n][:], compare_op=ALU.not_equal, fill=1.0, base=0,
                                       pattern=[[-1, P]], channel_multiplier=1).then_inc(setup.sem, 1)
                pool.affine_select(out=g["tri_s"][:], in_=g["tri_s"][:], compare_op=ALU.is_ge, fill=-BIG, base=0,
                                   pattern=[[-1, P]], channel_multiplier=1).then_inc(setup.sem, 1)
                pool.affine_select(out=g["tri_t"][:], in_=g["tri_t"][:], compare_op=ALU.is_ge, fill=-BIG, base=0,
                                   pattern=[[1, P]], channel_multiplier=-1).then_inc(setup.sem, 1)
                pool.affine_select(out=g["tri"][:], in_=g["tri"][:], compare_op=ALU.is_gt, fill=0.0, base=0,
                                   pattern=[[1, 16], [-1, 16]], channel_multiplier=0).then_inc(setup.sem, 1)
                pool.wait_ge(setup.sem, base + 13)

        setup.base += 13
        loaded.base += 16
        stop = LAYERS

        def att(name, **cfg):
            w = [t[name + "_w" + n] for n in "qkvo" if name + "_w" + n in t]
            attention(nc, g, S, dict(name=name, w=w, vec=t[name + "_vec"], bo=t.get(name + "_bo"), **cfg))

        if stop >= 1:
            att("a0", heads=16, ln=1, relu=True)
        if stop >= 2:
            ffn(nc, g, S, dict(name="f0", experts=8, used=8, top=1, hidden=64, ln=2, gelu=ACT.Gelu, wg=t["f0_wg"],
                               w1=t["f0_w1"], w2=t["f0_w2"], gamma=t["f0_gamma"], beta=t["f0_beta"], b1=t["f0_b1"],
                               b2=t["f0_b2"]))
        if stop >= 3:
            att("a1", heads=16, ln=2, lnc=True, qbias=True, kbias=True, mask=True, proj=True)
        if stop >= 4:
            ffn(nc, g, S, dict(name="f1", experts=16, used=4, top=4, hidden=1024, ln=1, gelu=ACT.Gelu_apprx_tanh,
                               wg=t["f1_wg"], w1=t["f1_w1"], w2=t["f1_w2"],
                               lora={n: t["f1_" + n] for n in ("a1", "b1", "a2", "b2")}))
        if stop >= 5:
            att("a2", heads=16, ln=1, qbias=True, kbias=True, proj=True)
        if stop >= 6:
            att("a3", heads=16, ln=2, self=True, causal=True, proj=True)
            ffn(nc, g, S, dict(name="f2", experts=8, used=8, top=2, hidden=512, ln=1, gelu=ACT.Gelu, from_y=True,
                               wg=t["f2_wg"], w1=t["f2_w1"], w2=t["f2_w2"], gamma=t["f2_gamma"]))
        if stop >= 7:
            att("a4", heads=8, dh=64, ln=2, lnc=True, qbias=True, kbias=True, proj=True)
        out_rows = out.rearrange("(t p) d -> t p d", p=P)
        if stop >= 8:
            quantised_linear(nc, g, S, t["q_w"], t["q_bias"], out_rows)
        else:
            with nc.Block() as block:
                @block.sync
                def _(sp):
                    sp.dma_start(out.rearrange("(t p) d -> p t d", p=P), g["X"][:]).then_inc(loaded.sem, 16)
                    sp.wait_ge(loaded.sem, loaded.base + 16)


LAYERS = 8


def packed(inputs):
    import numpy as np
    a = {k: np.asarray(v) for k, v in inputs.items()}
    f = np.float32
    t = {"x": a["x"].reshape(TOK, D), "ctx": a["ctx_1024"].reshape(TOK, D), "mask": a["mask_BxS2_ik0"]}

    def tiles(w):
        k = w.shape[0] // P
        return w.reshape(k, P, -1).transpose(1, 0, 2).reshape(P, -1)

    def heads(w):
        r = w.shape[0]
        return w.reshape(r, 8, 2, 16).transpose(0, 2, 3, 1).reshape(r, -1)

    def column(v):
        return v.reshape(-1, P).T

    def layer(name, wq, wk, wv, wo=None, gq=None, bq=None, gk=None, bk=None, qb=None, kb=None, vb=None, bo=None,
              wide=False):
        C = wq.shape[1]
        order = (lambda w: w) if wide else heads
        one, zero, none = np.ones(D, f), np.zeros(D, f), np.zeros(C, f)

        def pick(v, other):
            return other if v is None else v

        t[name + "_wq"], t[name + "_wk"], t[name + "_wv"] = tiles(order(wq)), tiles(order(wk)), tiles(wv)
        t[name + "_vec"] = np.concatenate(
            [column(pick(gq, one)), column(pick(bq, zero)), column(pick(gk, one)), column(pick(bk, zero)),
             column(order(pick(qb, none)[None])[0]), column(order(pick(kb, none)[None])[0]),
             column(pick(vb, none))], axis=1)
        if wo is not None:
            t[name + "_wo"] = tiles(wo)
            t[name + "_bo"] = pick(bo, zero)[None]

    layer("a0", a["L0_xattn_Wq"].T, a["L0_xattn_Wk"].T, a["L0_xattn_Wv"].T)
    kv = a["L1_xattn_w_kv"]
    layer("a1", a["L1_xattn_w_q"], kv[:, :D], kv[:, D:], a["L1_xattn_w_proj"], a["L1_xattn_g_x"], a["L1_xattn_b_x"],
          a["L1_xattn_g_kv"], a["L1_xattn_b_kv"], bo=a["L1_xattn_b_proj"])
    layer("a2", a["L2_xattn_Wq"], a["L2_xattn_Wk"], a["L2_xattn_Wv"], a["L2_xattn_Wo"], qb=a["L2_xattn_bq"],
          kb=a["L2_xattn_bk"], vb=a["L2_xattn_bv"], bo=a["L2_xattn_bo"])
    w = a["L2_ffn_c_attn_w"]
    layer("a3", w[:, :D], w[:, D:2 * D], w[:, 2 * D:], a["L2_ffn_c_proj_w"], gq=a["L2_ffn_ln1_w"],
          gk=a["L2_ffn_ln1_w"])
    kv = a["L3_xattn_Wkv"]
    layer("a4", a["L3_xattn_Wq"], kv[:, :2 * D], kv[:, 2 * D:], a["L3_xattn_Wout"], a["L3_xattn_g1"],
          a["L3_xattn_b1"], a["L3_xattn_g2"], a["L3_xattn_b2"], bo=a["L3_xattn_bout"], wide=True)

    E, _, H = a["L0_ffn_W1"].shape
    t["f0_wg"] = tiles(a["L0_ffn_Wg"].T)
    t["f0_w1"] = tiles(a["L0_ffn_W1"].transpose(1, 0, 2).reshape(D, E * H))
    pairs = np.zeros((E // 2, 2, H, 2, D), f)
    for i in range(2):
        pairs[:, i, :, i, :] = a["L0_ffn_W2"].reshape(E // 2, 2, H, D)[:, i]
    t["f0_w2"] = pairs.reshape(E // 2, P, 2 * D).transpose(1, 0, 2).reshape(P, -1)
    t["f0_gamma"], t["f0_beta"] = tiles(a["L0_ffn_ln_scale"].T), tiles(a["L0_ffn_ln_bias"].T)
    t["f0_b1"] = a["L0_ffn_b1"].reshape(E // 2, P).T
    t["f0_b2"] = a["L0_ffn_b2"]

    n = 4
    t["f1_wg"] = tiles(a["L1_ffn_Wg"])
    t["f1_w1"] = tiles(a["L1_ffn_W1"][:n].transpose(1, 0, 2).reshape(D, -1))
    t["f1_w2"] = tiles(a["L1_ffn_W2"][:n].reshape(-1, D))
    t["f1_a1"] = a["L1_ffn_A1"][:n].transpose(2, 0, 1).reshape(16, -1)
    t["f1_b1"] = a["L1_ffn_B1"][:n].transpose(1, 0, 2).reshape(16, -1)
    t["f1_a2"] = a["L1_ffn_A2"][:n].transpose(2, 0, 1).reshape(16, -1)
    t["f1_b2"] = a["L1_ffn_B2"][:n].transpose(1, 0, 2).reshape(16, -1)

    t["f2_wg"] = tiles(a["L2_ffn_router_w"])
    t["f2_w1"] = tiles(a["L2_ffn_w1"])
    t["f2_w2"] = tiles(a["L2_ffn_w2"])
    t["f2_gamma"] = column(a["L2_ffn_ln2_w"])

    t["q_w"] = tiles(a["L3_ffn_weight"].T)
    t["q_bias"] = a["L3_ffn_bias"][None]
    return {k: np.ascontiguousarray(v) for k, v in t.items()}


def kernel(**inputs):
    import concourse.bacc as bacc
    from concourse.bass_utils import run_bass_kernel_spmd

    nc = bacc.Bacc("TRN2", target_bir_lowering=False, num_devices=1)
    arrays = packed(inputs)
    t = {k: nc.dram_tensor("in_" + k, v.shape, mybir.dt.from_np(v.dtype), kind="ExternalInput").ap()
         for k, v in arrays.items()}
    out = nc.dram_tensor("out", (TOK, D), F32, kind="ExternalOutput").ap()
    network(nc, t, out)
    r = run_bass_kernel_spmd(nc, [{"in_" + k: v for k, v in arrays.items()}], core_ids=[0])
    return r.results[0]["out"].reshape(BATCH, SEQ, D)
```
